# Optimizing a Trainium2 kernel written in Bass

```python
import numpy as np
import jax
import jax.numpy as jnp

def _softmax(x, axis=-1):
    return jax.nn.softmax(x, axis=axis)

def _gelu(x):
    return jax.nn.gelu(x, approximate=True)

def _silu(x):
    return jax.nn.silu(x)

def _sigmoid(x):
    return jax.nn.sigmoid(x)

def _layernorm(x, axis=-1, eps=1e-05):
    m = jnp.mean(x, axis=axis, keepdims=True)
    v = jnp.var(x, axis=axis, keepdims=True)
    return (x - m) / jnp.sqrt(v + eps)

def _scatter_add(tgt, idx, src, axis=0):
    return tgt.at[idx].add(src)

def _segment_sum(src, seg, n):
    return jax.ops.segment_sum(src, seg, n)
kernel_name = 'mk_adj_ffn_d1_adj_r2_6b087c'

def setup_inputs(seed: int=0):
    np.random.seed(seed)
    _w = jnp.asarray

    def _rec_inputs():
        import jax
        import jax.numpy as jnp
        _gk = jax.random.key(seed)
        x = 7.22e-05 + 1 * jax.random.normal(jax.random.fold_in(_gk, 1), (128, 64, 256), jnp.float32)
        _w = (1.0 + jnp.arange(64, dtype=jnp.float32)) ** (-0.5)
        _w = _w / _w.mean()
        _pij = jnp.clip(0.0625 * _w[:, None] * _w[None, :], 0.0, 1.0)
        _a = jax.random.uniform(jax.random.fold_in(_gk, 2), (128, 64, 64)) < _pij
        _a = jnp.logical_or(_a, jnp.swapaxes(_a, -1, -2))
        _a = jnp.logical_or(_a, jnp.eye(64, dtype=bool))
        _af = _a.astype(jnp.float32)
        _af = _af * jax.random.uniform(jax.random.fold_in(_gk, 3), (128, 64, 64), jnp.float32, 0.05, 1)
        adj = _af
        return (x, adj)
    x, adj = _rec_inputs()

    def _L0_gnn_setup():
        import jax, jax.numpy as jnp
        import numpy as np
        EMBED_DIM = 256
        NUM_HEADS = 8
        HEAD_DIM = EMBED_DIM // NUM_HEADS
        SCALE = HEAD_DIM ** (-0.5)
        B, S = (16, 512)
        key = jax.random.key(seed)
        ks = jax.random.split(key, 12)
        init = lambda k, shape: jax.random.normal(k, shape, dtype=jnp.float32) * EMBED_DIM ** (-0.5)
        return {'x': jax.random.normal(ks[0], (B, S, EMBED_DIM), dtype=jnp.float32), 'adj_matrix': jax.random.uniform(ks[1], (B, S, S), dtype=jnp.float32), 'bond_matrix': jax.random.uniform(ks[2], (B, S, S), dtype=jnp.float32), 'Wq': init(ks[3], (EMBED_DIM, EMBED_DIM)), 'bq': jnp.zeros((EMBED_DIM,), jnp.float32), 'Wk': init(ks[4], (EMBED_DIM, EMBED_DIM)), 'bk': jnp.zeros((EMBED_DIM,), jnp.float32), 'Wv': init(ks[5], (EMBED_DIM, EMBED_DIM)), 'bv': jnp.zeros((EMBED_DIM,), jnp.float32), 'Wo': init(ks[6], (EMBED_DIM, EMBED_DIM)), 'bo': jnp.zeros((EMBED_DIM,), jnp.float32), 'seq_len': S}
    _L0_gnn_all = _L0_gnn_setup()
    _L0_gnn_in = {k: v for k, v in _L0_gnn_all.items() if k in ('Wq', 'bq', 'Wk', 'bk', 'Wv', 'bv', 'Wo', 'bo')}
    del _L0_gnn_all

    def _L0_ffn_setup():
        import jax, jax.numpy as jnp
        import numpy as np
        EPS = 1e-05
        TOP_K = 2

        def _moe_forward(x, Wg, W1, b1, W2, b2, gamma, beta):
            B, S, D = x.shape
            xf = x.reshape(-1, D)
            logits = xf @ Wg
            topv, topi = jax.lax.top_k(logits, TOP_K)
            gate_w = jax.nn.softmax(topv, axis=-1)
            h = jax.nn.relu(jnp.einsum('td,edh->teh', xf, W1) + b1[None])
            y = jnp.einsum('teh,ehd->ted', h, W2) + b2[None]
            mu = jnp.mean(y, axis=-1, keepdims=True)
            var = jnp.mean((y - mu) ** 2, axis=-1, keepdims=True)
            y = (y - mu) / jnp.sqrt(var + EPS) * gamma[None] + beta[None]
            y_sel = jnp.take_along_axis(y, topi[:, :, None], axis=1)
            out = jnp.sum(gate_w[:, :, None] * y_sel, axis=1)
            return out.reshape(B, S, D)
        key = jax.random.key(seed)
        ks = jax.random.split(key, 8)
        B, S, D, H, E = (4, 1024, 256, 256, 8)
        sd = lambda fan_in: 1.0 / np.sqrt(fan_in)
        x = jax.random.normal(ks[0], (B, S, D), dtype=jnp.float32)
        Wg = jax.random.uniform(ks[1], (D, E), jnp.float32, -sd(D), sd(D))
        W1 = jax.random.uniform(ks[2], (E, D, H), jnp.float32, -sd(D), sd(D))
        b1 = jax.random.uniform(ks[3], (E, H), jnp.float32, -sd(D), sd(D))
        W2 = jax.random.uniform(ks[4], (E, H, D), jnp.float32, -sd(H), sd(H))
        b2 = jax.random.uniform(ks[5], (E, D), jnp.float32, -sd(H), sd(H))
        gamma = jnp.ones((E, D), jnp.float32)
        beta = jnp.zeros((E, D), jnp.float32)
        return {'x': x, 'Wg': Wg, 'W1': W1, 'b1': b1, 'W2': W2, 'b2': b2, 'gamma': gamma, 'beta': beta}
    _L0_ffn_all = _L0_ffn_setup()
    _L0_ffn_in = {k: v for k, v in _L0_ffn_all.items() if k in ('Wg', 'W1', 'b1', 'W2', 'b2', 'gamma', 'beta')}
    del _L0_ffn_all
    return {'x': x, 'adj': adj, 'L0_gnn_Wq': _L0_gnn_in['Wq'], 'L0_gnn_bq': _L0_gnn_in['bq'], 'L0_gnn_Wk': _L0_gnn_in['Wk'], 'L0_gnn_bk': _L0_gnn_in['bk'], 'L0_gnn_Wv': _L0_gnn_in['Wv'], 'L0_gnn_bv': _L0_gnn_in['bv'], 'L0_gnn_Wo': _L0_gnn_in['Wo'], 'L0_gnn_bo': _L0_gnn_in['bo'], 'L0_ffn_Wg': _L0_ffn_in['Wg'], 'L0_ffn_W1': _L0_ffn_in['W1'], 'L0_ffn_b1': _L0_ffn_in['b1'], 'L0_ffn_W2': _L0_ffn_in['W2'], 'L0_ffn_b2': _L0_ffn_in['b2'], 'L0_ffn_gamma': _L0_ffn_in['gamma'], 'L0_ffn_beta': _L0_ffn_in['beta']}

def reference(x, adj, L0_gnn_Wq, L0_gnn_bq, L0_gnn_Wk, L0_gnn_bk, L0_gnn_Wv, L0_gnn_bv, L0_gnn_Wo, L0_gnn_bo, L0_ffn_Wg, L0_ffn_W1, L0_ffn_b1, L0_ffn_W2, L0_ffn_b2, L0_ffn_gamma, L0_ffn_beta):
    import jax
    import jax.numpy as jnp

    def _L0_gnn_ref(x, adj_matrix, bond_matrix, Wq, bq, Wk, bk, Wv, bv, Wo, bo, seq_len):
        import jax, jax.numpy as jnp
        import numpy as np
        EMBED_DIM = 256
        NUM_HEADS = 8
        HEAD_DIM = EMBED_DIM // NUM_HEADS
        SCALE = HEAD_DIM ** (-0.5)
        B, S = (16, 512)
        b = x.shape[0]

        def proj(W, bias):
            y = jnp.einsum('bse,fe->bsf', x, W) + bias
            return y.reshape(b, seq_len, NUM_HEADS, HEAD_DIM).transpose(0, 2, 1, 3)
        q, k, v = (proj(Wq, bq), proj(Wk, bk), proj(Wv, bv))
        scores = jnp.einsum('bhqd,bhkd->bhqk', q, k) * SCALE
        mask = (adj_matrix + bond_matrix)[:, None, :, :]
        scores = scores * mask
        attn = jax.nn.softmax(scores, axis=-1)
        ctx = jnp.einsum('bhqk,bhkd->bhqd', attn, v)
        ctx = ctx.transpose(0, 2, 1, 3).reshape(b, seq_len, EMBED_DIM)
        return jnp.einsum('bse,fe->bsf', ctx, Wo) + bo

    def _L0_ffn_ref(x, Wg, W1, b1, W2, b2, gamma, beta):
        import jax, jax.numpy as jnp
        import numpy as np
        EPS = 1e-05
        TOP_K = 2

        def _moe_forward(x, Wg, W1, b1, W2, b2, gamma, beta):
            B, S, D = x.shape
            xf = x.reshape(-1, D)
            logits = xf @ Wg
            topv, topi = jax.lax.top_k(logits, TOP_K)
            gate_w = jax.nn.softmax(topv, axis=-1)
            h = jax.nn.relu(jnp.einsum('td,edh->teh', xf, W1) + b1[None])
            y = jnp.einsum('teh,ehd->ted', h, W2) + b2[None]
            mu = jnp.mean(y, axis=-1, keepdims=True)
            var = jnp.mean((y - mu) ** 2, axis=-1, keepdims=True)
            y = (y - mu) / jnp.sqrt(var + EPS) * gamma[None] + beta[None]
            y_sel = jnp.take_along_axis(y, topi[:, :, None], axis=1)
            out = jnp.sum(gate_w[:, :, None] * y_sel, axis=1)
            return out.reshape(B, S, D)
        return _moe_forward(x, Wg, W1, b1, W2, b2, gamma, beta)
    x = x + _L0_gnn_ref(_layernorm(x, axis=-1), adj, adj, L0_gnn_Wq, L0_gnn_bq, L0_gnn_Wk, L0_gnn_bk, L0_gnn_Wv, L0_gnn_bv, L0_gnn_Wo, L0_gnn_bo, 64)
    x = x + _L0_ffn_ref(_layernorm(x, axis=-1), L0_ffn_Wg, L0_ffn_W1, L0_ffn_b1, L0_ffn_W2, L0_ffn_b2, L0_ffn_gamma, L0_ffn_beta)
    return x

_drawn_inputs = setup_inputs


def setup_inputs(seed=0):
    import zlib

    import numpy as np

    out = dict(_drawn_inputs(seed))
    spreads = {'L0_gnn_bq': (0.0, 0.1),
     'L0_gnn_bk': (0.0, 0.1),
     'L0_gnn_bv': (0.0, 0.1),
     'L0_gnn_bo': (0.0, 0.1),
     'L0_ffn_gamma': (1.0, 0.2),
     'L0_ffn_beta': (0.0, 0.1)}
    factors = {}
    for name, (base, spread) in spreads.items():
        noise = np.random.default_rng([zlib.crc32(name.encode()), seed]).standard_normal(out[name].shape)
        drawn = base * np.exp(spread * noise) if base else spread * noise
        out[name] = jnp.asarray(drawn.astype(out[name].dtype))
    for name, factor in factors.items():
        out[name] = (out[name] * factor).astype(out[name].dtype)
    return out
```

```python
from contextlib import ExitStack

import concourse.bass as bass
from concourse import mybir

F32 = mybir.dt.float32
BF16 = mybir.dt.bfloat16
I32 = mybir.dt.int32
U32 = mybir.dt.uint32
ALU = mybir.AluOpType
ACT = mybir.ActivationFunctionType
AX_X = mybir.AxisListType.X

P = 128
EPS = 1e-5


def gnn_moe_layer_kernel(nc, x, adj, Wq, bq, Wk, bk, Wv, bv, Wo, bo, Wg, W1, b1, W2, b2, gamma, beta, out):
    B, S, D = x.shape
    H = 8
    Dh = D // H
    SCALE = float(Dh) ** -0.5
    E, _, F = W1.shape
    T = B * S
    KC = D // P
    BJ = 4
    BT = BJ * P
    NBLK = T // BT
    NT = T // P
    R = 4
    GPT = P // S
    GT = 256
    GS = GT // P
    K = 2
    CARRY = 16
    ROW = D + CARRY
    CAP = T + GT
    CAPG = CAP // GT
    NG = (K * T - GT) // GT + E
    PAD0 = E * CAP
    assert D == 256 and F == 256 and E == 8 and S == 64 and KC == 2 and NG % 2 == 1
    assert K * T // GT + E >= NG

    xt = x.rearrange("b s d -> (b s) d").rearrange("(i j p) d -> i p j d", j=BJ, p=P)
    adjt = adj.rearrange("b s k -> (b s) k").rearrange("(i j p) k -> i p j k", j=BJ, p=P)
    outt = out.rearrange("b s d -> (b s) d").rearrange("(i j p) d -> i p j d", j=BJ, p=P)
    rows = nc.dram_tensor("expert_rows", [PAD0 + 2 * E * GT, ROW], F32, kind="Internal").ap()
    results = nc.dram_tensor("expert_results", [K * T + 2 * E * GT, D], F32, kind="Internal").ap()
    res_t = results[0:K * T, :].rearrange("(k i j p) d -> k i p j d", k=K, j=BJ, p=P)

    with ExitStack() as ctx:
        def sb(name, shape, dt=F32):
            return ctx.enter_context(nc.sbuf_tensor(name, shape, dt))

        def sem(name):
            return ctx.enter_context(nc.semaphore(name))

        bank = [ctx.enter_context(nc.psum_tensor(f"bank{n}", [P, 512], F32)) for n in range(8)]
        SBK = bank[0:4]
        W0, W1b, W2b = bank[4], bank[5], bank[7]
        RB = bank[6]

        ident = sb("ident", [P, P])
        upper = sb("upper", [P, P], BF16)
        ones = sb("ones", [P, P], BF16)
        iota_e = sb("iota_e", [P, E])
        base_e = sb("base_e", [P, E])
        ids = sb("ids", [P, NT, K], I32)
        small_rows = sb("small_rows", [22, P])
        cols = sb("cols", [P, 22])
        bvb = sb("bvb", [P, KC, P])
        boB = sb("boB", [P, D])
        wqT = sb("wqT", [P, KC, D])
        wkT = sb("wkT", [P, KC, D])
        wvT = sb("wvT", [P, KC, D])
        woT = sb("woT", [P, KC, D])
        wg = sb("wg", [P, KC, E])
        we = sb("we", [P, E, 4, 256])
        b2B = sb("b2B", [P, E, D])
        gaB = sb("gaB", [P, E, D])
        beB = sb("beB", [P, E, D])
        gates = sb("gates", [P, NT, K])
        x2 = sb("x2", [P, NT, D])

        xin = sb("xin", [P, BJ, D])
        adjs = sb("adjs", [P, BJ, S])
        xn = sb("xn", [P, BJ, D])
        xT = sb("xT", [P, KC, BT])
        qT = sb("qT", [P, KC, BT])
        kT = sb("kT", [P, KC, BT])
        vb = sb("vb", [P, BJ * GPT, R, 2, Dh])
        sm = sb("sm", [P, R, BT])
        mx = sb("mx", [P, R, 8])
        sums = sb("sums", [P, R, 8])
        pT = sb("pT", [P, R, BT])
        cT = sb("cT", [P, KC, BT])
        row = sb("row", [P, BJ, K, ROW])
        hT2 = sb("hT2", [P, KC, BT])
        st = sb("st", [P, BJ, 6])
        mv = sb("mv", [P, BJ, 2])
        var = sb("var", [P, BJ])
        lnv = sb("lnv", [P, BJ])
        rs0 = sb("rs0", [P, BJ])
        tmp = sb("tmp", [P, BJ])
        rstd = sb("rstd", [P, BJ])
        lg = sb("lg", [P, BJ, E])
        top = sb("top", [P, BJ, 8])
        topi = sb("topi", [P, BJ, 8], U32)
        e12 = sb("e12", [P, BJ, K])
        hot = sb("hot", [P, BJ, K, E])
        both = sb("both", [P, BJ, E], BF16)
        run = sb("run", [P, E])
        runb = sb("runb", [P, E], BF16)
        blk = sb("blk", [P, E])
        place = sb("place", [P, BJ, E])
        sel = sb("sel", [P, BJ, K, E])
        dstf = sb("dstf", [P, BJ * K])
        dst = sb("dst", [P, BJ * K], I32)
        gd = sb("gd", [P, BJ])
        gx = sb("gx", [P, BJ])
        gs = sb("gs", [P, BJ])

        cnt = sb("cnt", [P, E])
        ngi = sb("ngi", [P, E], I32)
        ngf = sb("ngf", [P, E])
        one8 = sb("one8", [P, E])
        onesf = sb("onesf", [1, P])
        cum = sb("cum", [P, E])
        iota_g = sb("iota_g", [1, NG])
        ge = sb("ge", [1, NG, E])
        gg = sb("gg", [1, NG, E])
        gexp = sb("gexp", [1, NG])
        gprev = sb("gprev", [1, NG])
        tabf = sb("tabf", [1, 2, NG])
        tab = sb("tab", [1, 2, NG], I32)
        padf = sb("padf", [1, E])
        padi = sb("padi", [1, E], I32)
        pad_ids = sb("pad_ids", [P, 2 * E, GS, CARRY], I32)
        zrow = sb("zrow", [P, D])
        yidx = [sb("yidx0", [P, GS], I32), sb("yidx1", [P, GS], I32)]
        yst = sb("yst", [P, GS, 6])
        ymv = sb("ymv", [P, GS, 2])
        yva = sb("yva", [P, GS])
        yln = sb("yln", [P, GS])
        yr0 = sb("yr0", [P, GS])
        ytm = sb("ytm", [P, GS])
        yrs = sb("yrs", [P, GS])

        setup_in = sem("setup_in")
        experts_in = sem("experts_in")
        pads_out = sem("pads_out")
        consts = sem("consts")
        dconst = sem("dconst")
        wo_perm = sem("wo_perm")
        su_pe = sem("su_pe")
        su_act = sem("su_act")
        bvb_done = sem("bvb_done")
        waits_passed = sem("waits_passed")
        x_in = sem("x_in")
        adj_in = sem("adj_in")
        adj_scaled = sem("adj_scaled")
        xbo_done = sem("xbo_done")
        ln1_s = sem("ln1_s")
        ln2_s = sem("ln2_s")
        var_done = sem("var_done")
        lnv_done = sem("lnv_done")
        rs0_done = sem("rs0_done")
        xn_done = sem("xn_done")
        xT_ps = sem("xT_ps")
        xT_done = sem("xT_done")
        qk_ps = sem("qk_ps")
        qk_done = sem("qk_done")
        v_ps = sem("v_ps")
        v_done = sem("v_done")
        s_ps = sem("s_ps")
        masked = sem("masked")
        mx_done = sem("mx_done")
        sub_done = sem("sub_done")
        exp_done = sem("exp_done")
        sum_s = sem("sum_s")
        rsum_done = sem("rsum_done")
        prob_done = sem("prob_done")
        pT_ps = sem("pT_ps")
        pT_done = sem("pT_done")
        c_ps = sem("c_ps")
        c_done = sem("c_done")
        o_ps = sem("o_ps")
        res_done = sem("res_done")
        row_done = sem("row_done")
        row2_done = sem("row2_done")
        h_ps = sem("h_ps")
        h_done = sem("h_done")
        lg_ps = sem("lg_ps")
        rt = sem("rt")
        both_done = sem("both_done")
        place_ps = sem("place_ps")
        gd_done = sem("gd_done")
        gx_done = sem("gx_done")
        dst_done = sem("dst_done")
        ids_done = sem("ids_done")
        scattered = sem("scattered")
        cnt_ps = sem("cnt_ps")
        tb = sem("tb")
        tab_done = sem("tab_done")
        g_in = [sem("g_in0"), sem("g_in1")]
        w_cur = sem("w_cur")
        gT_ps = sem("gT_ps")
        gT_done = sem("gT_done")
        m_ps = sem("m_ps")
        m_done = sem("m_done")
        y_ps = sem("y_ps")
        yb = sem("yb")
        y_read = sem("y_read")
        yvar = sem("yvar")
        ylnv = sem("ylnv")
        yrs0 = sem("yrs0")
        yn_done = sem("yn_done")
        yidx_done = sem("yidx_done")
        yg_done = sem("yg_done")
        yo_done = sem("yo_done")
        y_out = sem("y_out")
        r_in = [sem("r_in0"), sem("r_in1")]
        f_s = sem("f_s")
        f_done = sem("f_done")
        o_out = sem("o_out")

        wc = [vb[:, :, :, :, :].rearrange("p a b c d -> p (a b c d)")[:, 0:1024].rearrange("p (k f) -> p k f", k=4),
              vb[:, :, :, :, :].rearrange("p a b c d -> p (a b c d)")[:, 1024:2048].rearrange("p (k f) -> p k f", k=4)]
        smf = sm[:, :, :].rearrange("p a b -> p (a b)")
        pTf = pT[:, :, :].rearrange("p a b -> p (a b)")
        gin = [smf[:, 0:GS * ROW].rearrange("p (s w) -> p s w", s=GS),
               smf[:, 1024:1024 + GS * ROW].rearrange("p (s w) -> p s w", s=GS)]
        gT = xT[:, :, 0:GT]
        mT = qT[:, :, 0:GT]
        ybuf = [kT[:, 0, :].rearrange("p (s d) -> p s d", s=GS), kT[:, 1, :].rearrange("p (s d) -> p s d", s=GS)]
        yout = [pTf[:, 0:512].rearrange("p (s d) -> p s d", s=GS), pTf[:, 512:1024].rearrange("p (s d) -> p s d", s=GS)]
        rbuf = [[xin, xn], [cT[:, :, :].rearrange("p a (b d) -> p (a b) d", d=D),
                            hT2[:, :, :].rearrange("p a (b d) -> p (a b) d", d=D)]]

        def wait_apart(eng, sem_, value):
            eng.wait_ge(sem_, value)
            eng.sem_inc(waits_passed, 1)

        block = ctx.enter_context(nc.Block())
        SETUP_LOADS = 4 + 3 + KC + 2
        EXPERT_LOADS = 4 + 3
        SU_BO = 6
        RT = 15
        NCONST = 11

        @block.sync
        def _(sp):
            def load(dst_, src_):
                sp.dma_start(dst_, src_).then_inc(setup_in, 16)

            sp.dma_start(xin[:, :, :], xt[0]).then_inc(x_in, 16)
            sp.dma_start(adjs[:, :, :], adjt[0]).then_inc(adj_in, 16)
            for n, w in enumerate((Wq, Wk, Wv, Wo)):
                load(pTf[:, 512 * n:512 * n + 512].rearrange("p (c e) -> p c e", c=KC),
                     w.rearrange("(c p) e -> p c e", p=P))
            load(small_rows[0:16, :], b1.rearrange("e (c p) -> (e c) p", p=P))
            load(small_rows[16:18, :], bq.rearrange("(c p) -> c p", p=P))
            load(small_rows[18:20, :], bk.rearrange("(c p) -> c p", p=P))
            bvv = bv.rearrange("(hh c r d) -> c r hh d", hh=2, c=2, r=2)
            for c in range(KC):
                load(small_rows[20 + c:21 + c, :].rearrange("o (r hh d) -> o r hh d", r=2, hh=2), bvv[c:c + 1])
            load(boB[0:1, :], bo.rearrange("(o n) -> o n", o=1))
            load(wg[:, :, :], Wg.rearrange("(c p) e -> p c e", p=P))
            def load_expert(dst_, src_):
                sp.dma_start(dst_, src_).then_inc(experts_in, 16)

            for c in range(2):
                load_expert(we[:, :, c, :], W1[:, c * P:(c + 1) * P, :].rearrange("e p f -> p e f"))
                load_expert(we[:, :, 2 + c, :], W2[:, c * P:(c + 1) * P, :].rearrange("e p f -> p e f"))
            load_expert(b2B[:, :, :], b2.partition_broadcast(P))
            load_expert(gaB[:, :, :], gamma.partition_broadcast(P))
            load_expert(beB[:, :, :], beta.partition_broadcast(P))
            sp.wait_ge(consts, NCONST)
            padv = rows[PAD0:PAD0 + 2 * E * GT, :].rearrange("(s p) w -> p s w", p=P)
            sp.dma_start(padv[:, :, 0:D], zrow[:, :].unsqueeze(1).to_broadcast([P, 2 * E * GS, D])).then_inc(pads_out, 16)
            sp.dma_start(padv[:, :, D:ROW], pad_ids[:, :, :, :].bitcast(F32).rearrange("p a s w -> p (a s) w")).then_inc(pads_out, 16)

            with sp.Fori(1, NBLK) as i:
                sp.wait_ge(xn_done, i)
                sp.wait_ge(xbo_done, i)
                sp.dma_start(xin[:, :, :], xt[bass.ds(i, 1)].rearrange("o p j d -> (o p) j d")).then_inc(x_in, 16)
                sp.wait_ge(masked, R * i)
                sp.dma_start(adjs[:, :, :], adjt[bass.ds(i, 1)].rearrange("o p j d -> (o p) j d")).then_inc(adj_in, 16)

            sp.wait_ge(tab_done, 1)
            sp.wait_ge(scattered, 16 * BJ * K * NBLK)
            sp.wait_ge(pads_out, 32)
            for e in range(E):
                at = sp.value_load(padi[0:1, e:e + 1], min_val=e * CAP, max_val=e * CAP + T)
                sp.dma_start(rows[bass.ds(at, GT), :], rows[PAD0 + (E + e) * GT:PAD0 + (E + e + 1) * GT, :]).then_inc(pads_out, 16)
            sp.wait_ge(pads_out, 32 + 16 * E)

            def load_group(g, b):
                at = sp.value_load(tab[0:1, 0, bass.ds(g, 1)], min_val=0, max_val=PAD0 + (E - 1) * GT)
                sp.dma_start(gin[b], rows[bass.ds(at, GT), :].rearrange("(s p) w -> p s w", p=P)).then_inc(g_in[b], 16)

            def next_group(g, n, b):
                sp.wait_ge(gT_ps, n)
                sp.wait_ge(yidx_done, n)
                load_group(g, b)

            load_group(0, 0)
            load_group(1, 1)
            with sp.Fori(0, (NG - 3) // 2) as m:
                next_group(2 * m + 2, 2 * m + 1, 0)
                next_group(2 * m + 3, 2 * m + 2, 1)
            next_group(NG - 1, NG - 2, 0)
            sp.wait_ge(y_out, GS * 16 * NG)

            def load_results(i, b):
                for k in range(K):
                    sp.dma_start(rbuf[b][k][:, :, :], res_t[k][bass.ds(i, 1)].rearrange("o p j d -> (o p) j d")).then_inc(r_in[b], 16)

            load_results(0, 0)
            load_results(1, 1)
            with sp.Fori(0, NBLK // 2 - 1) as m:
                for b in range(2):
                    sp.wait_ge(f_done, 2 * m + b + 1)
                    sp.dma_start(outt[bass.ds(2 * m + b, 1)].rearrange("o p j d -> (o p) j d"),
                                 x2[:, bass.ds((2 * m + b) * BJ, BJ), :]).then_inc(o_out, 16)
                    load_results(2 * m + b + 2, b)
            for i in range(NBLK - 2, NBLK):
                sp.wait_ge(f_done, i + 1)
                sp.dma_start(outt[i], x2[:, i * BJ:(i + 1) * BJ, :]).then_inc(o_out, 16)
            sp.wait_ge(o_out, 16 * NBLK)
            sp.wait_ge(pads_out, 32 + 16 * E)

        @block.gpsimd
        def _(pool):
            def const(ins):
                ins.then_inc(consts, 1)

            const(pool.memset(ident[:, :], 0.0))
            const(pool.memset(ones[:, :], 1.0))
            const(pool.memset(zrow[:, :], 0.0))
            const(pool.memset(row[:, :, :, D:ROW], 0.0))
            const(pool.iota(ids[:, :, :], pattern=[[P, NT], [T, K]], base=0, channel_multiplier=1))
            const(pool.iota(pad_ids[:, :, :, :], pattern=[[GT, 2 * E], [P, GS], [0, CARRY]], base=K * T, channel_multiplier=1))
            const(pool.iota(iota_e[:, :], pattern=[[1, E]], base=0, channel_multiplier=0, allow_small_or_imprecise_dtypes=True))
            const(pool.iota(iota_g[:, :], pattern=[[1, NG]], base=0, channel_multiplier=0, allow_small_or_imprecise_dtypes=True))
            pool.wait_ge(consts, 8)
            const(pool.affine_select(out=ident[:, :], in_=ident[:, :], compare_op=ALU.not_equal, fill=1.0,
                                     base=0, pattern=[[-1, P]], channel_multiplier=1))
            const(pool.affine_select(out=upper[:, :], in_=ones[:, :], compare_op=ALU.is_gt, fill=0.0,
                                     base=0, pattern=[[1, P]], channel_multiplier=-1))
            const(pool.tensor_scalar(base_e[:, :], iota_e[:, :], float(CAP), None, ALU.mult))

            def scale_mask(i):
                wait_apart(pool, adj_in, 16 * i + 16)
                pool.tensor_scalar(adjs[:, :, :], adjs[:, :, :], 2.0 * SCALE, None, ALU.mult).then_inc(adj_scaled, 1)

            def x_plus_bo(i):
                wait_apart(pool, x_in, 16 * i + 16)
                pool.tensor_tensor(x2[:, bass.ds(i * BJ, BJ), :], xin[:, :, :],
                                   boB[:, :].unsqueeze(1).to_broadcast([P, BJ, D]), ALU.add).then_inc(xbo_done, 1)

            def sub_max(i):
                for r in range(R):
                    wait_apart(pool, mx_done, R * i + r + 1)
                    v = sm[:, r, :].rearrange("p (a k) -> p a k", k=S)
                    pool.tensor_tensor(v, v, mx[:, r, :].unsqueeze(2).to_broadcast([P, 8, S]), ALU.subtract).then_inc(sub_done, 1)

            def normalise(i):
                for r in range(R):
                    wait_apart(pool, rsum_done, R * i + r + 1)
                    v = sm[:, r, :].rearrange("p (a k) -> p a k", k=S)
                    pool.tensor_tensor(v, v, sums[:, r, :].unsqueeze(2).to_broadcast([P, 8, S]), ALU.mult).then_inc(prob_done, 1)

            def carry(i):
                if not isinstance(i, int) or i > 0:
                    wait_apart(pool, scattered, 16 * BJ * K * i)
                pool.tensor_copy(row[:, :, :, D:D + 1].bitcast(I32).rearrange("p j k o -> p j (k o)"),
                                 ids[:, bass.ds(i * BJ, BJ), :]).then_inc(ids_done, 1)

            def scatter(i):
                wait_apart(pool, ids_done, i + 1)
                wait_apart(pool, dst_done, i + 1)
                wait_apart(pool, row_done, i + 1)
                wait_apart(pool, row2_done, i + 1)
                for j in range(BJ):
                    for k in range(K):
                        n = j * K + k
                        pool.indirect_dma_start(rows, bass.IndirectOffsetOnAxis(dst[:, n:n + 1], 0), row[:, j, k, :], None,
                                                bounds_check=PAD0 - 1, oob_is_err=False).then_inc(scattered, 16)

            def body(i, first, last):
                if not last:
                    x_plus_bo(i + 1)
                sub_max(i)
                if not last:
                    wait_apart(pool, masked, R * i + R)
                    scale_mask(i + 1)
                if not first:
                    carry(i - 1)
                normalise(i)
                if not first:
                    scatter(i - 1)

            pool.wait_ge(consts, NCONST)
            scale_mask(0)
            pool.wait_ge(su_act, SU_BO)
            x_plus_bo(0)
            body(0, True, False)
            with pool.Fori(1, NBLK - 1) as i:
                body(i, False, False)
            body(NBLK - 1, False, True)
            carry(NBLK - 1)
            scatter(NBLK - 1)

            def take_places(n, nb, b, used=True):
                wait_apart(pool, g_in[b], 16 * nb + 16)
                if used:
                    wait_apart(pool, y_out, 16 * GS * (n - 1))
                pool.tensor_copy(yidx[b][:, :], gin[b][:, :, D:D + 1].bitcast(I32).rearrange("p s o -> p (s o)")).then_inc(yidx_done, 1)

            def finish(n, b):
                pool.wait_ge(tab_done, 1)
                e = pool.value_load(tab[0:1, 1, bass.ds(n, 1)], min_val=0, max_val=E - 1)
                wait_apart(pool, yn_done, n + 1)
                pool.tensor_tensor(yout[b], yout[b], gaB[:, bass.ds(e, 1), :].to_broadcast([P, GS, D]), ALU.mult).then_inc(yg_done, 1)
                wait_apart(pool, yg_done, n + 1)
                pool.tensor_tensor(yout[b], yout[b], beB[:, bass.ds(e, 1), :].to_broadcast([P, GS, D]), ALU.add).then_inc(yo_done, 1)
                wait_apart(pool, yo_done, n + 1)
                wait_apart(pool, yidx_done, n + 1)
                for s in range(GS):
                    pool.indirect_dma_start(results, bass.IndirectOffsetOnAxis(yidx[b][:, s:s + 1], 0), yout[b][:, s, :], None,
                                            bounds_check=K * T + 2 * E * GT - 1, oob_is_err=False).then_inc(y_out, 16)

            wait_apart(pool, scattered, 16 * BJ * K * NBLK)
            take_places(0, 0, 0, used=False)
            with pool.Fori(0, (NG - 1) // 2) as m:
                take_places(2 * m + 1, m, 1)
                finish(2 * m, 0)
                take_places(2 * m + 2, m + 1, 0)
                finish(2 * m + 1, 1)
            finish(NG - 1, 0)
            pool.wait_ge(y_out, 16 * GS * NG)

        @block.vector
        def _(dve):
            dve.memset(vb[:, :, :, :, :].rearrange("p a b c d -> p (a b c d)"), 0.0).then_inc(dconst, 1)
            dve.memset(onesf[:, :], 1.0).then_inc(dconst, 1)
            dve.memset(one8[:, :], 1.0).then_inc(dconst, 1)
            dve.memset(run[:, :], 0.0).then_inc(dconst, 1)
            dve.memset(runb[:, :], 0.0).then_inc(dconst, 1)
            dve.wait_ge(setup_in, 16 * SETUP_LOADS)
            wo_nat = pTf[:, 1536:2048].rearrange("p (f hh c r d) -> p f c r hh d", f=KC, hh=2, c=KC, r=2)
            for f in range(KC):
                for c in range(KC):
                    o = smf[:, (f * KC + c) * P:(f * KC + c + 1) * P].rearrange("p (r hh d) -> p r hh d", r=2, hh=2)
                    ins = dve.tensor_copy(o, wo_nat[:, f, c])
            ins.then_inc(wo_perm, 1)
            dve.wait_ge(su_act, 1)
            for c in range(KC):
                ins = dve.tensor_copy(bvb[:, c, :], cols[:, 20 + c:21 + c].to_broadcast([P, P]))
            ins.then_inc(bvb_done, 1)

            LN = 6

            def layernorm(n, src, which, s, out_, done):
                c = 0
                for j in range(BJ):
                    ins = dve.bn_stats(st[:, j, :], src(j))
                ins.then_inc(s, 1)
                wait_apart(dve, s, LN * n + 1)
                for j in range(BJ):
                    ins = dve.bn_aggr(mv[:, j, :], st[:, j, :])
                ins.then_inc(s, 1)
                dve.wait_ge(s, LN * n + 2)
                dve.tensor_scalar(var[:, :], mv[:, :, 1], EPS, None, ALU.add).then_inc(var_done, 1)
                dve.wait_ge(rs0_done, which(n))
                dve.tensor_tensor(tmp[:, :], var[:, :], rs0[:, :], ALU.mult).then_inc(s, 1)
                dve.wait_ge(s, LN * n + 3)
                dve.tensor_tensor(tmp[:, :], tmp[:, :], rs0[:, :], ALU.mult).then_inc(s, 1)
                dve.wait_ge(s, LN * n + 4)
                dve.tensor_scalar(tmp[:, :], tmp[:, :], -0.5, 1.5, ALU.mult, ALU.add).then_inc(s, 1)
                dve.wait_ge(s, LN * n + 5)
                dve.tensor_tensor(rstd[:, :], tmp[:, :], rs0[:, :], ALU.mult).then_inc(s, 1)
                dve.wait_ge(s, LN * n + 6)
                for j in range(BJ):
                    ins = dve.tensor_scalar(out_(j), src(j), mv[:, j, 0:1], rstd[:, j:j + 1], ALU.subtract, ALU.mult)
                ins.then_inc(done, 1)

            def ln1(i):
                if not isinstance(i, int) or i > 0:
                    dve.wait_ge(xT_ps, KC * i)
                wait_apart(dve, x_in, 16 * i + 16)
                layernorm(i, lambda j: xin[:, j, :], lambda n: LN1_AT(n), ln1_s, lambda j: xn[:, j, :], xn_done)

            def LN1_AT(n):
                if isinstance(n, int):
                    return 1 if n == 0 else 2 * n
                return 2 * n

            def LN2_AT(n):
                if isinstance(n, int) and n == NBLK - 1:
                    return 2 * NBLK
                return 2 * n + 3

            def ln2(i):
                if not isinstance(i, int) or i > 0:
                    wait_apart(dve, scattered, 16 * BJ * K * i)
                layernorm(i, lambda j: x2[:, bass.ds(i * BJ + j, 1), :].rearrange("p o d -> p (o d)"), lambda n: LN2_AT(n),
                          ln2_s, lambda j: row[:, j, 0, 0:D], row_done)

            def mask_and_max(i):
                dve.wait_ge(adj_scaled, i + 1)
                dve.wait_ge(s_ps, i + 1)
                for r in range(R):
                    a = adjs[:, :, :].unsqueeze(2).to_broadcast([P, BJ, 2, S])
                    dve.tensor_tensor(sm[:, r, :].rearrange("p (j h k) -> p j h k", j=BJ, h=2),
                                      SBK[r][:, :].rearrange("p (j h k) -> p j h k", j=BJ, h=2), a, ALU.mult).then_inc(masked, 1)
                for r in range(R):
                    dve.wait_ge(masked, R * i + r + 1)
                    dve.tensor_reduce(mx[:, r, :], sm[:, r, :].rearrange("p (a k) -> p a k", k=S), AX_X, ALU.max).then_inc(mx_done, 1)

            def prob_sums(i):
                for r in range(R):
                    dve.wait_ge(exp_done, R * i + r + 1)
                    dve.tensor_reduce(sums[:, r, :], sm[:, r, :].rearrange("p (a k) -> p a k", k=S), AX_X, ALU.add).then_inc(sum_s, 1)
                    dve.wait_ge(sum_s, R * i + r + 1)
                    dve.reciprocal(sums[:, r, :], sums[:, r, :]).then_inc(rsum_done, 1)

            def route_a(i):
                n = 0
                dve.wait_ge(lg_ps, i + 1)
                dve.tensor_copy(lg[:, :, :].rearrange("p j e -> p (j e)"), RB[:, 0:BJ * E]).then_inc(rt, 1)
                wait_apart(dve, rt, RT * i + 1)
                for j in range(BJ):
                    ins = dve.max(top[:, j, :], lg[:, j, :])
                ins.then_inc(rt, 1)
                wait_apart(dve, rt, RT * i + 2)
                for j in range(BJ):
                    ins = dve.max_index(topi[:, j, :], top[:, j, :], lg[:, j, :])
                ins.then_inc(rt, 1)
                dve.tensor_tensor(gd[:, :], top[:, :, 1], top[:, :, 0], ALU.subtract).then_inc(gd_done, 1)
                dve.wait_ge(rt, RT * i + 3)
                dve.tensor_copy(e12[:, :, :], topi[:, :, 0:K]).then_inc(rt, 1)
                dve.wait_ge(rt, RT * i + 4)
                dve.tensor_tensor(hot[:, :, :, :].rearrange("p j k e -> p (j k) e"),
                                  iota_e[:, :].unsqueeze(1).to_broadcast([P, BJ * K, E]),
                                  e12[:, :, :].rearrange("p j k -> p (j k)").unsqueeze(2).to_broadcast([P, BJ * K, E]),
                                  ALU.is_equal).then_inc(rt, 1)
                dve.wait_ge(rt, RT * i + 5)
                dve.tensor_tensor(both[:, :, :], hot[:, :, 0, :], hot[:, :, 1, :], ALU.add).then_inc(both_done, 1)

            def route_b(i):
                dve.wait_ge(place_ps, i + 1)
                dve.tensor_tensor(place[:, :, :], RB[:, 64:64 + BJ * E].rearrange("p (j e) -> p j e", j=BJ),
                                  base_e[:, :].unsqueeze(1).to_broadcast([P, BJ, E]), ALU.add).then_inc(rt, 1)
                dve.tensor_reduce(blk[:, :], both[:, :, :].rearrange("p j e -> p e j"), AX_X, ALU.add).then_inc(rt, 1)
                dve.wait_ge(rt, RT * i + 6)
                dve.tensor_tensor(sel[:, :, :, :], hot[:, :, :, :], place[:, :, :].unsqueeze(2).to_broadcast([P, BJ, K, E]),
                                  ALU.mult).then_inc(rt, 1)
                dve.wait_ge(rt, RT * i + 7)
                dve.tensor_tensor(run[:, :], run[:, :], blk[:, :], ALU.add).then_inc(rt, 1)
                dve.wait_ge(rt, RT * i + 8)
                dve.tensor_reduce(dstf[:, :], sel[:, :, :, :].rearrange("p j k e -> p (j k) e"), AX_X, ALU.add).then_inc(rt, 1)
                dve.wait_ge(rt, RT * i + 9)
                dve.tensor_copy(runb[:, :], run[:, :]).then_inc(rt, 1)
                dve.wait_ge(rt, RT * i + 10)
                if not isinstance(i, int) or i > 0:
                    dve.wait_ge(scattered, 16 * BJ * K * i)
                dve.tensor_copy(dst[:, :], dstf[:, :]).then_inc(dst_done, 1)
                dve.wait_ge(gx_done, i + 1)
                dve.tensor_scalar(gs[:, :], gx[:, :], 1.0, None, ALU.add).then_inc(rt, 1)
                dve.wait_ge(rt, RT * i + 12)
                dve.reciprocal(gs[:, :], gs[:, :]).then_inc(rt, 1)
                dve.wait_ge(rt, RT * i + 13)
                dve.tensor_copy(gates[:, bass.ds(i * BJ, BJ), 0:1].rearrange("p j o -> p (j o)"), gs[:, :]).then_inc(rt, 1)
                dve.tensor_tensor(gates[:, bass.ds(i * BJ, BJ), 1:2].rearrange("p j o -> p (j o)"), gx[:, :], gs[:, :], ALU.mult).then_inc(rt, 1)

            def residual(i):
                for jj in range(2):
                    dve.wait_ge(xbo_done, i + 1)
                    dve.wait_ge(o_ps, 2 * i + jj + 1)
                    v = x2[:, bass.ds(i * BJ + 2 * jj, 2), :].rearrange("p j d -> p (j d)")
                    ins = dve.tensor_tensor(v, (W0, W1b)[jj][:, :], v, ALU.add)
                    ins.then_inc(res_done, 1)
                wait_apart(dve, res_done, 2 * i + 2)

            def body(i, first, last):
                if not last:
                    ln1(i + 1)
                mask_and_max(i)
                if not first:
                    route_a(i - 1)
                prob_sums(i)
                if not first:
                    route_b(i - 1)
                residual(i)
                ln2(i)

            ln1(0)
            body(0, True, False)
            with dve.Fori(1, NBLK - 1) as i:
                body(i, False, False)
            body(NBLK - 1, False, True)
            route_a(NBLK - 1)
            route_b(NBLK - 1)

            tn = [0]

            def t(ins):
                tn[0] += 1
                ins.then_inc(tb, 1)
                dve.wait_ge(tb, tn[0])

            dve.wait_ge(cnt_ps, 1)
            t(dve.tensor_copy(cnt[:, :], RB[:, 0:E]))
            t(dve.tensor_scalar(ngf[:, :], cnt[:, :], float(GT - 1), None, ALU.add))
            t(dve.tensor_copy(ngi[:, :], ngf[:, :]))
            t(dve.tensor_scalar(ngi[:, :], ngi[:, :], GT.bit_length() - 1, None, ALU.logical_shift_right))
            t(dve.tensor_copy(ngf[:, :], ngi[:, :]))
            t(dve.tensor_tensor_scan(cum[:, :], one8[:, :], ngf[:, :], 0.0, ALU.mult, ALU.add))
            t(dve.tensor_tensor(padf[:, :], cnt[0:1, :], base_e[0:1, :], ALU.add))
            t(dve.tensor_copy(padi[:, :], padf[:, :]))
            t(dve.tensor_tensor(ge[:, :, :], iota_g[:, :].unsqueeze(2).to_broadcast([1, NG, E]),
                                cum[0:1, :].unsqueeze(1).to_broadcast([1, NG, E]), ALU.is_ge))
            t(dve.tensor_tensor(gg[:, :, :], ge[:, :, :], ngf[0:1, :].unsqueeze(1).to_broadcast([1, NG, E]), ALU.mult))
            t(dve.tensor_reduce(gexp[:, :], ge[:, :, :], AX_X, ALU.add))
            t(dve.tensor_reduce(gprev[:, :], gg[:, :, :], AX_X, ALU.add))
            t(dve.tensor_scalar(tabf[:, 0, :], gexp[:, :], float(CAPG), None, ALU.mult))
            t(dve.tensor_tensor(tabf[:, 0, :], tabf[:, 0, :], gprev[:, :], ALU.subtract))
            t(dve.tensor_tensor(tabf[:, 0, :], tabf[:, 0, :], iota_g[:, :], ALU.add))
            t(dve.tensor_scalar(tabf[:, 0, :], tabf[:, 0, :], float(GT), None, ALU.mult))
            t(dve.tensor_scalar(tabf[:, 1, :], gexp[:, :], float(E - 1), None, ALU.min))
            dve.tensor_copy(tab[:, :, :], tabf[:, :, :]).then_inc(tab_done, 1)

            YS = 9

            def group(n, b, used=True):
                e = dve.value_load(tab[0:1, 1, bass.ds(n, 1)], min_val=0, max_val=E - 1)
                dve.wait_ge(y_ps, n + 1)
                dve.tensor_tensor(ybuf[b], RB[:, :].rearrange("p (s d) -> p s d", s=GS),
                                  b2B[:, bass.ds(e, 1), :].to_broadcast([P, GS, D]), ALU.add).then_inc(y_read, 1)
                wait_apart(dve, y_read, n + 1)
                for q in range(GS):
                    ins = dve.bn_stats(yst[:, q, :], ybuf[b][:, q, :])
                ins.then_inc(yb, 1)
                wait_apart(dve, yb, 6 * n + 1)
                for q in range(GS):
                    ins = dve.bn_aggr(ymv[:, q, :], yst[:, q, :])
                ins.then_inc(yb, 1)
                dve.wait_ge(yb, 6 * n + 2)
                dve.tensor_scalar(yva[:, :], ymv[:, :, 1], EPS, None, ALU.add).then_inc(yvar, 1)
                dve.wait_ge(yrs0, n + 1)
                dve.tensor_tensor(ytm[:, :], yva[:, :], yr0[:, :], ALU.mult).then_inc(yb, 1)
                dve.wait_ge(yb, 6 * n + 3)
                dve.tensor_tensor(ytm[:, :], ytm[:, :], yr0[:, :], ALU.mult).then_inc(yb, 1)
                dve.wait_ge(yb, 6 * n + 4)
                dve.tensor_scalar(ytm[:, :], ytm[:, :], -0.5, 1.5, ALU.mult, ALU.add).then_inc(yb, 1)
                dve.wait_ge(yb, 6 * n + 5)
                dve.tensor_tensor(yrs[:, :], ytm[:, :], yr0[:, :], ALU.mult).then_inc(yb, 1)
                dve.wait_ge(yb, 6 * n + 6)
                if used:
                    dve.wait_ge(y_out, 16 * GS * (n - 1))
                for q in range(GS):
                    ins = dve.tensor_scalar(yout[b][:, q, :], ybuf[b][:, q, :], ymv[:, q, 0:1], yrs[:, q:q + 1], ALU.subtract, ALU.mult)
                ins.then_inc(yn_done, 1)

            dve.wait_ge(tab_done, 1)
            dve.wait_ge(experts_in, 16 * EXPERT_LOADS)
            group(0, 0, used=False)
            group(1, 1, used=False)
            with dve.Fori(1, (NG - 1) // 2) as m:
                group(2 * m, 0)
                group(2 * m + 1, 1)
            group(NG - 1, 0)

            def combine(i, nb, b):
                dve.wait_ge(r_in[b], 16 * K * (nb + 1))
                for k in range(K):
                    for j in range(BJ):
                        v = x2[:, bass.ds(i * BJ + j, 1), :].rearrange("p o d -> p (o d)")
                        g = gates[:, bass.ds(i * BJ + j, 1), k:k + 1].rearrange("p o k -> p (o k)")
                        ins = dve.scalar_tensor_tensor(v, rbuf[b][k][:, j, :], g, v, ALU.mult, ALU.add)
                    if k == 0:
                        ins.then_inc(f_s, 1)
                        dve.wait_ge(f_s, i + 1)
                ins.then_inc(f_done, 1)

            with dve.Fori(0, NBLK // 2) as m:
                combine(2 * m, m, 0)
                combine(2 * m + 1, m, 1)

        @block.scalar
        def _(act):
            nc.scalar.preload_act_table_set("natural_log_exp_and_others")

            def copy(o, i_, sem_):
                act.activation(o, i_, ACT.Copy).then_inc(sem_, 1)

            act.wait_ge(su_pe, 1)
            copy(cols[:, :], W0[:, 0:22], su_act)
            for n, w in enumerate((wqT, wkT, wvT, woT)):
                act.wait_ge(su_pe, n + 2)
                copy(w[:, :, :].rearrange("p c f -> p (c f)"), SBK[n][:, :], su_act)
            act.wait_ge(su_pe, 6)
            copy(boB[:, :], W1b[:, 0:D], su_act)

            def rsqrt_start(n):
                act.wait_ge(var_done, n + 1)
                act.activation(lnv[:, :], var[:, :], ACT.Ln).then_inc(lnv_done, 1)
                act.wait_ge(lnv_done, n + 1)
                act.activation(rs0[:, :], lnv[:, :], ACT.Exp, scale=-0.5).then_inc(rs0_done, 1)

            def x_copies(i):
                for c in range(KC):
                    act.wait_ge(xT_ps, KC * i + c + 1)
                    copy(xT[:, c, :], (W2b, W0)[c][:, :], xT_done)

            def qk_copy(i, m):
                act.wait_ge(qk_ps, 4 * i + m + 1)
                act.activation((qT, kT)[m // 2][:, m % 2, :], (W1b, W2b, W0, W1b)[m][:, :], ACT.Identity,
                               bias=cols[:, 16 + m:17 + m]).then_inc(qk_done, 1)

            def exps(i, r):
                act.wait_ge(sub_done, R * i + r + 1)
                act.activation(sm[:, r, :], sm[:, r, :], ACT.Exp).then_inc(exp_done, 1)

            def v_copies(i):
                for jj in range(2):
                    act.wait_ge(v_ps, 2 * i + jj + 1)
                    for g in range(GPT):
                        for hh in range(2):
                            src = (W1b, W2b)[jj][S * g:S * g + S, :].rearrange("p (j h r d) -> p j h r d", j=2, h=2, r=R)[:, :, hh]
                            o = vb[S * hh:S * hh + S, :, :, hh, :].rearrange("p (j g) r d -> p j g r d", g=GPT)[:, 2 * jj:2 * jj + 2, g]
                            ins = act.activation(o, src, ACT.Copy)
                    ins.then_inc(v_done, 1)

            def h_copies(i):
                for c in range(KC):
                    act.wait_ge(h_ps, KC * i + c + 1)
                    copy(hT2[:, c, :], (W0, W1b)[c][:, :], h_done)

            def body(i, first, last):
                if not last:
                    rsqrt_start(2 * i + 1)
                if not first:
                    h_copies(i - 1)
                if not last:
                    x_copies(i + 1)
                for r in range(R):
                    if not last:
                        qk_copy(i + 1, r)
                    exps(i, r)
                if not first:
                    act.wait_ge(gd_done, i)
                    act.activation(gx[:, :], gd[:, :], ACT.Exp).then_inc(gx_done, 1)
                for r in range(R):
                    act.wait_ge(pT_ps, R * i + r + 1)
                    copy(pT[:, r, :], SBK[r][:, :], pT_done)
                for c in range(KC):
                    act.wait_ge(c_ps, KC * i + c + 1)
                    copy(cT[:, c, :], (W2b, W0)[c][:, :], c_done)
                if not last:
                    v_copies(i + 1)
                rsqrt_start(2 * i + 2 if not last else 2 * i + 1)
                act.wait_ge(row_done, i + 1)
                act.activation(row[:, :, 1, 0:D], row[:, :, 0, 0:D], ACT.Copy).then_inc(row2_done, 1)

            rsqrt_start(0)
            act.wait_ge(dconst, 5)
            x_copies(0)
            for m in range(4):
                qk_copy(0, m)
            v_copies(0)
            body(0, True, False)
            with act.Fori(1, NBLK - 1) as i:
                body(i, False, False)
            body(NBLK - 1, False, True)
            h_copies(NBLK - 1)
            act.wait_ge(gd_done, NBLK)
            act.activation(gx[:, :], gd[:, :], ACT.Exp).then_inc(gx_done, 1)

            def weights(n, b, used=True):
                e = act.value_load(tab[0:1, 1, bass.ds(n, 1)], min_val=0, max_val=E - 1)
                if used:
                    act.wait_ge(y_ps, n - 1)
                act.activation(wc[b], we[:, bass.ds(e, 1), :, :].rearrange("p o k f -> p (o k) f"), ACT.Copy).then_inc(w_cur, 1)

            def g_copy(n):
                act.wait_ge(gT_ps, n + 1)
                act.activation(gT, W0[:, :].rearrange("p (k t) -> p k t", k=KC), ACT.Copy).then_inc(gT_done, 1)

            def hidden(n):
                e = act.value_load(tab[0:1, 1, bass.ds(n, 1)], min_val=0, max_val=E - 1)
                for c in range(2):
                    act.wait_ge(m_ps, 2 * n + c + 1)
                    act.activation(mT[:, c, :], (W1b, W2b)[c][:, 0:GT], ACT.Relu, bias=cols[:, bass.ds(e * 2 + c, 1)]).then_inc(m_done, 1)

            def y_rsqrt(n):
                act.wait_ge(yvar, n + 1)
                act.activation(yln[:, :], yva[:, :], ACT.Ln).then_inc(ylnv, 1)
                act.wait_ge(ylnv, n + 1)
                act.activation(yr0[:, :], yln[:, :], ACT.Exp, scale=-0.5).then_inc(yrs0, 1)

            def step(n, b, more=True):
                g_copy(n + 1)
                if more:
                    weights(n + 2, b)
                hidden(n + 1)
                y_rsqrt(n)

            act.wait_ge(tab_done, 1)
            act.wait_ge(experts_in, 16 * EXPERT_LOADS)
            weights(0, 0, used=False)
            weights(1, 1, used=False)
            g_copy(0)
            hidden(0)
            with act.Fori(0, (NG - 3) // 2) as m:
                step(2 * m, 0)
                step(2 * m + 1, 1)
            step(NG - 3, 0)
            step(NG - 2, 1, more=False)
            y_rsqrt(NG - 1)

        @block.tensor
        def _(pe):
            pe.wait_ge(consts, NCONST)
            pe.wait_ge(setup_in, 16 * SETUP_LOADS)
            pe.transpose(W0[:, 0:22], small_rows[:, :], ident[0:22, 0:22]).then_inc(su_pe, 1)
            for n in range(4):
                if n == 3:
                    pe.wait_ge(wo_perm, 1)
                nat = (pTf[:, 512 * n:512 * n + 512] if n < 3 else smf[:, 0:512]).rearrange("p (f e) -> p f e", f=KC)
                for c in range(KC):
                    for f in range(KC):
                        mm = pe.transpose(SBK[n][:, c * D + f * P:c * D + (f + 1) * P], nat[:, f, c * P:(c + 1) * P], ident[:, :])
                mm.then_inc(su_pe, 1)
            pe.wait_ge(bvb_done, 1)
            pe.wait_ge(su_act, 5)
            pe.wait_ge(dconst, 5)
            for c in range(KC):
                pe.matmul(W1b[:, 0:D], bvb[:, c, :], woT[:, c, :], start=(c == 0), stop=False)
            pe.matmul(W1b[:, 0:D], onesf[:, :], boB[0:1, :], start=False, stop=True).then_inc(su_pe, 1)
            pe.wait_ge(su_act, 6)

            def x_transposes(i):
                pe.wait_ge(xn_done, i + 1)
                for c in range(KC):
                    if not isinstance(i, int) or i > 0:
                        if c == 0:
                            pe.wait_ge(v_done, 2 * i)
                        elif not isinstance(i, int):
                            pe.wait_ge(h_done, KC * (i - 2) + 1)
                        else:
                            pe.wait_ge(qk_done, 3)
                    for j in range(BJ):
                        mm = pe.transpose((W2b, W0)[c][:, j * P:(j + 1) * P], xn[:, j, c * P:(c + 1) * P], ident[:, :])
                    mm.then_inc(xT_ps, 1)

            def qk(i):
                pe.wait_ge(xT_done, KC * i + KC)
                if not isinstance(i, int) or i > 1:
                    pe.wait_ge(h_done, KC * (i - 2) + 2)
                for m in range(4):
                    if m == 3:
                        pe.wait_ge(qk_done, 4 * i + 1)
                    for c in range(KC):
                        mm = pe.matmul((W1b, W2b, W0, W1b)[m][:, :], (wqT, wkT)[m // 2][:, c, (m % 2) * P:(m % 2 + 1) * P],
                                       xT[:, c, :], start=(c == 0), stop=(c == KC - 1))
                    mm.then_inc(qk_ps, 1)

            def v(i):
                for jj in range(2):
                    if jj == 0:
                        pe.wait_ge(qk_done, 4 * i + 4)
                    elif not isinstance(i, int) or i > 0:
                        pe.wait_ge(c_done, KC * (i - 1) + 1)
                    for j in range(2):
                        t0 = (2 * jj + j) * P
                        for c in range(KC):
                            mm = pe.matmul((W1b, W2b)[jj][:, j * D:(j + 1) * D], xT[:, c, t0:t0 + P], wvT[:, c, :],
                                           start=(c == 0), stop=(c == KC - 1))
                    mm.then_inc(v_ps, 1)

            def scores(i):
                pe.wait_ge(qk_done, 4 * i + 4)
                if not isinstance(i, int) or i > 0:
                    pe.wait_ge(pT_done, R * i)
                for j in range(BJ):
                    for g in range(GPT):
                        t0 = j * P + g * S
                        for hh in range(2):
                            for r in range(R):
                                mm = pe.matmul(SBK[r][S * g:S * g + S, (2 * j + hh) * S:(2 * j + hh + 1) * S],
                                               qT[Dh * r:Dh * r + Dh, hh, t0:t0 + S], kT[Dh * r:Dh * r + Dh, hh, t0:t0 + S],
                                               start=True, stop=True)
                mm.then_inc(s_ps, 1)

            def row_transposes(i):
                pe.wait_ge(row_done, i + 1)
                for c in range(KC):
                    for j in range(BJ):
                        mm = pe.transpose((W0, W1b)[c][:, j * P:(j + 1) * P], row[:, j, 0, c * P:(c + 1) * P], ident[:, :])
                    mm.then_inc(h_ps, 1)

            def logits(i):
                pe.wait_ge(h_done, KC * i + KC)
                for j in range(BJ):
                    for c in range(KC):
                        mm = pe.matmul(RB[:, j * E:(j + 1) * E], hT2[:, c, j * P:(j + 1) * P], wg[:, c, :],
                                       start=(c == 0), stop=(c == KC - 1))
                mm.then_inc(lg_ps, 1)

            def places(i):
                pe.wait_ge(both_done, i + 1)
                o = RB[:, 64:64 + BJ * E]
                pe.matmul(o, upper[:, :], both[:, :, :].rearrange("p j e -> p (j e)"), start=True, stop=False, skip_group_check=True)
                for j in range(BJ - 1):
                    w = BJ - 1 - j
                    pe.matmul(RB[:, 64 + (j + 1) * E:64 + BJ * E].rearrange("p (j e) -> p j e", j=w), ones[:, :],
                              both[:, j, :].unsqueeze(1).to_broadcast([P, w, E]), start=False, stop=False, skip_group_check=True)
                pe.matmul(o.rearrange("p (j e) -> p j e", j=BJ), ones[:, :], runb[:, :].unsqueeze(1).to_broadcast([P, BJ, E]),
                          start=False, stop=True, skip_group_check=True).then_inc(place_ps, 1)

            def prob_transposes(i):
                for r in range(R):
                    pe.wait_ge(prob_done, R * i + r + 1)
                    for j in range(BJ):
                        mm = pe.transpose(SBK[r][:, j * P:(j + 1) * P], sm[:, r, j * P:(j + 1) * P], ident[:, :])
                    mm.then_inc(pT_ps, 1)

            def context(i, last):
                for c in range(KC):
                    pe.wait_ge(pT_done, R * i + 2 * c + 2)
                    if c == 0:
                        pe.wait_ge(v_done, 2 * i + 2)
                    if not last:
                        pe.wait_ge(qk_done, 4 * i + 4 + 2 + c)
                    elif c == 1:
                        pe.wait_ge(h_done, KC * (i - 1) + 1)
                    for j in range(BJ):
                        for g in range(GPT):
                            t0 = j * P + g * S
                            for r2 in range(2):
                                mm = pe.matmul((W2b, W0)[c][S * r2:S * r2 + S, t0:t0 + S],
                                               vb[:, 2 * j + g, 2 * c + r2, :, :].rearrange("p h d -> p (h d)"),
                                               pT[:, 2 * c + r2, t0:t0 + S], start=True, stop=True)
                    mm.then_inc(c_ps, 1)

            def output(i, last):
                pe.wait_ge(c_done, KC * i + KC)
                for jj in range(2):
                    if jj == 1:
                        if last:
                            pe.wait_ge(h_done, KC * i)
                        else:
                            pe.wait_ge(v_done, 2 * i + 3)
                    for j in range(2):
                        t0 = (2 * jj + j) * P
                        for c in range(KC):
                            mm = pe.matmul((W0, W1b)[jj][:, j * D:(j + 1) * D], cT[:, c, t0:t0 + P], woT[:, c, :],
                                           start=(c == 0), stop=(c == KC - 1))
                    mm.then_inc(o_ps, 1)

            def body(i, first, last):
                scores(i)
                if not first:
                    row_transposes(i - 1)
                    logits(i - 1)
                if not last:
                    x_transposes(i + 1)
                    qk(i + 1)
                if not first:
                    places(i - 1)
                prob_transposes(i)
                context(i, last)
                if not last:
                    v(i + 1)
                output(i, last)

            x_transposes(0)
            qk(0)
            v(0)
            body(0, True, False)
            with pe.Fori(1, NBLK - 1) as i:
                body(i, False, False)
            body(NBLK - 1, False, True)
            row_transposes(NBLK - 1)
            logits(NBLK - 1)
            places(NBLK - 1)
            pe.wait_ge(rt, RT * NBLK)
            pe.matmul(RB[:, 0:E], ones[:, :], runb[:, :], start=True, stop=True).then_inc(cnt_ps, 1)

            def group_transposes(n, nb, b):
                pe.wait_ge(g_in[b], 16 * (nb + 1))
                if not isinstance(n, int) or n > 0:
                    pe.wait_ge(gT_done, n)
                for c in range(KC):
                    for s in range(GS):
                        mm = pe.transpose(W0[:, c * GT + s * P:c * GT + (s + 1) * P], gin[b][:, s, c * P:(c + 1) * P], ident[:, :])
                mm.then_inc(gT_ps, 1)

            def layer1(n, b):
                pe.wait_ge(gT_done, n + 1)
                pe.wait_ge(w_cur, n + 1)
                if not isinstance(n, int) or n > 0:
                    pe.wait_ge(m_done, 2 * n)
                for m in range(2):
                    for c in range(KC):
                        mm = pe.matmul((W1b, W2b)[m][:, 0:GT], wc[b][:, c, m * P:(m + 1) * P], gT[:, c, :], start=(c == 0), stop=(c == KC - 1))
                    mm.then_inc(m_ps, 1)

            def layer2(n, b):
                pe.wait_ge(m_done, 2 * n + 2)
                if not isinstance(n, int) or n > 0:
                    pe.wait_ge(y_read, n)
                for s in range(GS):
                    for c in range(2):
                        mm = pe.matmul(RB[:, s * D:(s + 1) * D], mT[:, c, s * P:(s + 1) * P], wc[b][:, 2 + c, :], start=(c == 0), stop=(c == 1))
                mm.then_inc(y_ps, 1)

            def step(n, nb, b):
                group_transposes(n + 1, nb, 1 - b)
                layer2(n, b)
                layer1(n + 1, 1 - b)

            group_transposes(0, 0, 0)
            layer1(0, 0)
            with pe.Fori(0, (NG - 1) // 2) as m:
                step(2 * m, m, 0)
                step(2 * m + 1, m + 1, 1)
            layer2(NG - 1, 0)


_INS = ["x", "adj", "L0_gnn_Wq", "L0_gnn_bq", "L0_gnn_Wk", "L0_gnn_bk", "L0_gnn_Wv", "L0_gnn_bv", "L0_gnn_Wo", "L0_gnn_bo",
        "L0_ffn_Wg", "L0_ffn_W1", "L0_ffn_b1", "L0_ffn_W2", "L0_ffn_b2", "L0_ffn_gamma", "L0_ffn_beta"]
_OUTS = [((128, 64, 256), "float32")]


def kernel(**inputs):
    import numpy as _np
    import concourse.bacc as _bacc
    from concourse import mybir as _mybir
    from concourse.bass_utils import run_bass_kernel_spmd as _run

    nc = _bacc.Bacc("TRN2", target_bir_lowering=False, num_devices=1)
    arrays, args = {}, []
    for name in _INS:
        a = _np.ascontiguousarray(inputs[name])
        arrays[f"in_{name}_dram"] = a
        args.append(nc.dram_tensor(f"in_{name}_dram", a.shape, _mybir.dt.from_np(a.dtype), kind="ExternalInput").ap())
    for i, (shape, dtype) in enumerate(_OUTS):
        dt = _mybir.dt.from_np(_np.dtype(dtype))
        args.append(nc.dram_tensor(f"out_{i}_dram", shape, dt, kind="ExternalOutput").ap())
    gnn_moe_layer_kernel(nc, *args)
    r = _run(nc, [arrays], core_ids=[0])
    got = tuple(r.results[0][f"out_{i}_dram"] for i in range(len(_OUTS)))
    return got[0]
```

```python
from contextlib import ExitStack

import concourse.bass as bass
from concourse import mybir

F32 = mybir.dt.float32
BF16 = mybir.dt.bfloat16
I32 = mybir.dt.int32
U32 = mybir.dt.uint32
ALU = mybir.AluOpType
ACT = mybir.ActivationFunctionType
AX_X = mybir.AxisListType.X

P = 128
EPS = 1e-5


def gnn_moe_layer_kernel(nc, x, adj, Wq, bq, Wk, bk, Wv, bv, Wo, bo, Wg, W1, b1, W2, b2, gamma, beta, out):
    B, S, D = x.shape
    H = 8
    Dh = D // H
    SCALE = float(Dh) ** -0.5
    E, _, F = W1.shape
    T = B * S
    KC = D // P
    BJ = 4
    BT = BJ * P
    NBLK = T // BT
    NT = T // P
    R = 4
    GPT = P // S
    GT = 256
    GS = GT // P
    K = 2
    CARRY = 16
    ROW = D + CARRY
    CAP = T + GT
    CAPG = CAP // GT
    NG = (K * T - GT) // GT + E
    PAD0 = E * CAP
    assert D == 256 and F == 256 and E == 8 and S == 64 and KC == 2 and NG % 2 == 1
    assert K * T // GT + E >= NG

    xt = x.rearrange("b s d -> (b s) d").rearrange("(i j p) d -> i p j d", j=BJ, p=P)
    adjt = adj.rearrange("b s k -> (b s) k").rearrange("(i j p) k -> i p j k", j=BJ, p=P)
    outt = out.rearrange("b s d -> (b s) d").rearrange("(i j p) d -> i p j d", j=BJ, p=P)
    rows = nc.dram_tensor("expert_rows", [PAD0 + 2 * E * GT, ROW], F32, kind="Internal").ap()
    results = nc.dram_tensor("expert_results", [K * T + 2 * E * GT, D], F32, kind="Internal").ap()
    res_t = results[0:K * T, :].rearrange("(k i j p) d -> k i p j d", k=K, j=BJ, p=P)

    with ExitStack() as ctx:
        def sb(name, shape, dt=F32):
            return ctx.enter_context(nc.sbuf_tensor(name, shape, dt))

        def sem(name):
            return ctx.enter_context(nc.semaphore(name))

        bank = [ctx.enter_context(nc.psum_tensor(f"bank{n}", [P, 512], F32)) for n in range(8)]
        SBK = bank[0:4]
        W0, W1b, W2b = bank[4], bank[5], bank[7]
        RB = bank[6]

        ident = sb("ident", [P, P])
        upper = sb("upper", [P, P], BF16)
        ones = sb("ones", [P, P], BF16)
        iota_e = sb("iota_e", [P, E])
        base_e = sb("base_e", [P, E])
        ids = sb("ids", [P, NT, K], I32)
        small_rows = sb("small_rows", [22, P])
        cols = sb("cols", [P, 22])
        bvb = sb("bvb", [P, KC, P])
        boB = sb("boB", [P, D])
        wqT = sb("wqT", [P, KC, D])
        wkT = sb("wkT", [P, KC, D])
        wvT = sb("wvT", [P, KC, D])
        woT = sb("woT", [P, KC, D])
        wg = sb("wg", [P, KC, E])
        we = sb("we", [P, E, 4, 256])
        b2B = sb("b2B", [P, E, D])
        gaB = sb("gaB", [P, E, D])
        beB = sb("beB", [P, E, D])
        gates = sb("gates", [P, NT, K])
        x2 = sb("x2", [P, NT, D])

        xin = sb("xin", [P, BJ, D])
        adjs = sb("adjs", [P, BJ, S])
        xn = sb("xn", [P, BJ, D])
        xT = sb("xT", [P, KC, BT])
        qT = sb("qT", [P, KC, BT])
        kT = sb("kT", [P, KC, BT])
        vb = sb("vb", [P, BJ * GPT, R, 2, Dh])
        sm = sb("sm", [P, R, BT])
        mx = sb("mx", [P, R, 8])
        sums = sb("sums", [P, R, 8])
        pT = sb("pT", [P, R, BT])
        cT = sb("cT", [P, KC, BT])
        row = sb("row", [P, BJ, K, ROW])
        hT2 = sb("hT2", [P, KC, BT])
        st = sb("st", [P, BJ, 6])
        mv = sb("mv", [P, BJ, 2])
        var = sb("var", [P, BJ])
        lnv = sb("lnv", [P, BJ])
        rs0 = sb("rs0", [P, BJ])
        tmp = sb("tmp", [P, BJ])
        rstd = sb("rstd", [P, BJ])
        lg = sb("lg", [P, BJ, E])
        top = sb("top", [P, BJ, 8])
        topi = sb("topi", [P, BJ, 8], U32)
        e12 = sb("e12", [P, BJ, K])
        hot = sb("hot", [P, BJ, K, E])
        both = sb("both", [P, BJ, E], BF16)
        run = sb("run", [P, E])
        runb = sb("runb", [P, E], BF16)
        blk = sb("blk", [P, E])
        place = sb("place", [P, BJ, E])
        sel = sb("sel", [P, BJ, K, E])
        dstf = sb("dstf", [P, BJ * K])
        dst = sb("dst", [P, BJ * K], I32)
        gd = sb("gd", [P, BJ])
        gx = sb("gx", [P, BJ])
        gs = sb("gs", [P, BJ])

        cnt = sb("cnt", [P, E])
        ngi = sb("ngi", [P, E], I32)
        ngf = sb("ngf", [P, E])
        one8 = sb("one8", [P, E])
        onesf = sb("onesf", [1, P])
        cum = sb("cum", [P, E])
        iota_g = sb("iota_g", [1, NG])
        ge = sb("ge", [1, NG, E])
        gg = sb("gg", [1, NG, E])
        gexp = sb("gexp", [1, NG])
        gprev = sb("gprev", [1, NG])
        tabf = sb("tabf", [1, 2, NG])
        tab = sb("tab", [1, 2, NG], I32)
        padf = sb("padf", [1, E])
        padi = sb("padi", [1, E], I32)
        pad_ids = sb("pad_ids", [P, 2 * E, GS, CARRY], I32)
        zrow = sb("zrow", [P, D])
        places_kept = sb("places_kept", [P, NG, GS], I32)
        yidx = [sb("yidx0", [P, GS], I32), sb("yidx1", [P, GS], I32)]
        yst = sb("yst", [P, GS, 6])
        ymv = sb("ymv", [P, GS, 2])
        yva = sb("yva", [P, GS])
        yln = sb("yln", [P, GS])
        yr0 = sb("yr0", [P, GS])
        ytm = sb("ytm", [P, GS])
        yrs = [sb("yrs0", [P, GS]), sb("yrs1", [P, GS])]

        setup_in = sem("setup_in")
        experts_in = sem("experts_in")
        pads_out = sem("pads_out")
        consts = sem("consts")
        dconst = sem("dconst")
        wo_perm = sem("wo_perm")
        su_pe = sem("su_pe")
        su_act = sem("su_act")
        bvb_done = sem("bvb_done")
        waits_passed = sem("waits_passed")
        x_in = sem("x_in")
        adj_in = sem("adj_in")
        adj_scaled = sem("adj_scaled")
        xbo_done = sem("xbo_done")
        ln1_s = sem("ln1_s")
        ln2_s = sem("ln2_s")
        var_done = sem("var_done")
        lnv_done = sem("lnv_done")
        rs0_done = sem("rs0_done")
        xn_done = sem("xn_done")
        xT_ps = sem("xT_ps")
        xT_done = sem("xT_done")
        qk_ps = sem("qk_ps")
        qk_done = sem("qk_done")
        v_ps = sem("v_ps")
        v_done = sem("v_done")
        s_ps = sem("s_ps")
        masked = sem("masked")
        mx_done = sem("mx_done")
        sub_done = sem("sub_done")
        exp_done = sem("exp_done")
        sum_s = sem("sum_s")
        rsum_done = sem("rsum_done")
        prob_done = sem("prob_done")
        pT_ps = sem("pT_ps")
        pT_done = sem("pT_done")
        c_ps = sem("c_ps")
        c_done = sem("c_done")
        o_ps = sem("o_ps")
        res_done = sem("res_done")
        row_done = sem("row_done")
        row2_done = sem("row2_done")
        h_ps = sem("h_ps")
        h_done = sem("h_done")
        lg_ps = sem("lg_ps")
        rt = sem("rt")
        both_done = sem("both_done")
        place_ps = sem("place_ps")
        gd_done = sem("gd_done")
        gx_done = sem("gx_done")
        dst_done = sem("dst_done")
        ids_done = sem("ids_done")
        scattered = sem("scattered")
        cnt_ps = sem("cnt_ps")
        tb = sem("tb")
        tab_done = sem("tab_done")
        g_in = [sem("g_in0"), sem("g_in1")]
        w_cur = [sem("w1_cur"), sem("w2_cur")]
        gT_ps = sem("gT_ps")
        gT_done = sem("gT_done")
        m_ps = sem("m_ps")
        m_done = sem("m_done")
        y_ps = sem("y_ps")
        yb = sem("yb")
        y_read = sem("y_read")
        yvar = sem("yvar")
        ylnv = sem("ylnv")
        yrs0 = sem("yrs0")
        yrs_done = sem("yrs_done")
        ys_done = sem("ys_done")
        kept = sem("kept")
        yidx_done = sem("yidx_done")
        yo_done = sem("yo_done")
        y_out = [sem("y_out0"), sem("y_out1")]
        r_in = [sem(f"r_in{b}") for b in range(4)]
        f_s = sem("f_s")
        f_done = sem("f_done")
        o_out = sem("o_out")

        vbf = vb[:, :, :, :, :].rearrange("p a b c d -> p (a b c d)")
        wc = [[vbf[:, 1024 * l + 512 * b:1024 * l + 512 * b + 512].rearrange("p (k f) -> p k f", k=2) for b in range(2)]
              for l in range(2)]
        smf = sm[:, :, :].rearrange("p a b -> p (a b)")
        pTf = pT[:, :, :].rearrange("p a b -> p (a b)")
        gin = [smf[:, 0:GS * ROW].rearrange("p (s w) -> p s w", s=GS),
               smf[:, 1024:1024 + GS * ROW].rearrange("p (s w) -> p s w", s=GS)]
        gT = [xT[:, :, 0:GT], xT[:, :, GT:2 * GT]]
        mT = [qT[:, :, 0:GT], qT[:, :, GT:2 * GT]]
        GTB, MB, YB = SBK[0:2], SBK[2:4], (W0, W1b)
        ybuf = [kT[:, 0, :].rearrange("p (s d) -> p s d", s=GS), kT[:, 1, :].rearrange("p (s d) -> p s d", s=GS)]
        yout = [pTf[:, 0:512].rearrange("p (s d) -> p s d", s=GS), pTf[:, 512:1024].rearrange("p (s d) -> p s d", s=GS)]
        NR = 4
        rbuf = [[xin, xn], [cT[:, :, :].rearrange("p a (b d) -> p (a b) d", d=D),
                            hT2[:, :, :].rearrange("p a (b d) -> p (a b) d", d=D)]]
        for flat in (smf, pTf):
            rbuf.append([flat[:, 1024 * k:1024 * k + 1024].rearrange("p (j d) -> p j d", d=D) for k in range(K)])

        def wait_apart(eng, sem_, value):
            eng.wait_ge(sem_, value)
            eng.sem_inc(waits_passed, 1)

        block = ctx.enter_context(nc.Block())
        SETUP_LOADS = 4 + 3 + KC + 2
        EXPERT_LOADS = 4 + 3
        SU_BO = 6
        RT = 15
        NCONST = 11

        @block.sync
        def _(sp):
            def load(dst_, src_):
                sp.dma_start(dst_, src_).then_inc(setup_in, 16)

            sp.dma_start(xin[:, :, :], xt[0]).then_inc(x_in, 16)
            sp.dma_start(adjs[:, :, :], adjt[0]).then_inc(adj_in, 16)
            for n, w in enumerate((Wq, Wk, Wv, Wo)):
                load(pTf[:, 512 * n:512 * n + 512].rearrange("p (c e) -> p c e", c=KC),
                     w.rearrange("(c p) e -> p c e", p=P))
            load(small_rows[0:16, :], b1.rearrange("e (c p) -> (e c) p", p=P))
            load(small_rows[16:18, :], bq.rearrange("(c p) -> c p", p=P))
            load(small_rows[18:20, :], bk.rearrange("(c p) -> c p", p=P))
            bvv = bv.rearrange("(hh c r d) -> c r hh d", hh=2, c=2, r=2)
            for c in range(KC):
                load(small_rows[20 + c:21 + c, :].rearrange("o (r hh d) -> o r hh d", r=2, hh=2), bvv[c:c + 1])
            load(boB[0:1, :], bo.rearrange("(o n) -> o n", o=1))
            load(wg[:, :, :], Wg.rearrange("(c p) e -> p c e", p=P))
            def load_expert(dst_, src_):
                sp.dma_start(dst_, src_).then_inc(experts_in, 16)

            for c in range(2):
                load_expert(we[:, :, c, :], W1[:, c * P:(c + 1) * P, :].rearrange("e p f -> p e f"))
                load_expert(we[:, :, 2 + c, :], W2[:, c * P:(c + 1) * P, :].rearrange("e p f -> p e f"))
            load_expert(b2B[:, :, :], b2.partition_broadcast(P))
            load_expert(gaB[:, :, :], gamma.partition_broadcast(P))
            load_expert(beB[:, :, :], beta.partition_broadcast(P))
            sp.wait_ge(consts, NCONST)
            padv = rows[PAD0:PAD0 + 2 * E * GT, :].rearrange("(s p) w -> p s w", p=P)
            sp.dma_start(padv[:, :, 0:D], zrow[:, :].unsqueeze(1).to_broadcast([P, 2 * E * GS, D])).then_inc(pads_out, 16)
            sp.dma_start(padv[:, :, D:ROW], pad_ids[:, :, :, :].bitcast(F32).rearrange("p a s w -> p (a s) w")).then_inc(pads_out, 16)

            with sp.Fori(1, NBLK) as i:
                sp.wait_ge(xn_done, i)
                sp.wait_ge(xbo_done, i)
                sp.dma_start(xin[:, :, :], xt[bass.ds(i, 1)].rearrange("o p j d -> (o p) j d")).then_inc(x_in, 16)
                sp.wait_ge(masked, R * i)
                sp.dma_start(adjs[:, :, :], adjt[bass.ds(i, 1)].rearrange("o p j d -> (o p) j d")).then_inc(adj_in, 16)

            sp.wait_ge(tab_done, 1)
            sp.wait_ge(scattered, 16 * BJ * K * NBLK)
            sp.wait_ge(pads_out, 32)
            for e in range(E):
                at = sp.value_load(padi[0:1, e:e + 1], min_val=e * CAP, max_val=e * CAP + T)
                sp.dma_start(rows[bass.ds(at, GT), :], rows[PAD0 + (E + e) * GT:PAD0 + (E + e + 1) * GT, :]).then_inc(pads_out, 16)
            sp.wait_ge(pads_out, 32 + 16 * E)

            def load_group(g, b):
                at = sp.value_load(tab[0:1, 0, bass.ds(g, 1)], min_val=0, max_val=PAD0 + (E - 1) * GT)
                sp.dma_start(gin[b], rows[bass.ds(at, GT), :].rearrange("(s p) w -> p s w", p=P)).then_inc(g_in[b], 16)

            def next_group(g, n, b):
                sp.wait_ge(gT_ps, n)
                sp.wait_ge(kept, n)
                load_group(g, b)

            load_group(0, 0)
            load_group(1, 1)
            with sp.Fori(0, (NG - 3) // 2) as m:
                next_group(2 * m + 2, 2 * m + 1, 0)
                next_group(2 * m + 3, 2 * m + 2, 1)
            next_group(NG - 1, NG - 2, 0)
            for b in range(2):
                sp.wait_ge(y_out[b], 16 * GS * ((NG + 1 - b) // 2))

            def load_results(i, b):
                for k in range(K):
                    sp.dma_start(rbuf[b][k][:, :, :], res_t[k][bass.ds(i, 1)].rearrange("o p j d -> (o p) j d")).then_inc(r_in[b], 16)

            for b in range(NR):
                load_results(b, b)
            with sp.Fori(0, NBLK // NR - 1) as m:
                for b in range(NR):
                    sp.wait_ge(f_done, NR * m + b + 1)
                    load_results(NR * m + b + NR, b)
            sp.wait_ge(pads_out, 32 + 16 * E)

        @block.gpsimd
        def _(pool):
            def const(ins):
                ins.then_inc(consts, 1)

            const(pool.memset(ident[:, :], 0.0))
            const(pool.memset(ones[:, :], 1.0))
            const(pool.memset(zrow[:, :], 0.0))
            const(pool.memset(row[:, :, :, D:ROW], 0.0))
            const(pool.iota(ids[:, :, :], pattern=[[P, NT], [T, K]], base=0, channel_multiplier=1))
            const(pool.iota(pad_ids[:, :, :, :], pattern=[[GT, 2 * E], [P, GS], [0, CARRY]], base=K * T, channel_multiplier=1))
            const(pool.iota(iota_e[:, :], pattern=[[1, E]], base=0, channel_multiplier=0, allow_small_or_imprecise_dtypes=True))
            const(pool.iota(iota_g[:, :], pattern=[[1, NG]], base=0, channel_multiplier=0, allow_small_or_imprecise_dtypes=True))
            pool.wait_ge(consts, 8)
            const(pool.affine_select(out=ident[:, :], in_=ident[:, :], compare_op=ALU.not_equal, fill=1.0,
                                     base=0, pattern=[[-1, P]], channel_multiplier=1))
            const(pool.affine_select(out=upper[:, :], in_=ones[:, :], compare_op=ALU.is_gt, fill=0.0,
                                     base=0, pattern=[[1, P]], channel_multiplier=-1))
            const(pool.tensor_scalar(base_e[:, :], iota_e[:, :], float(CAP), None, ALU.mult))

            def scale_mask(i):
                wait_apart(pool, adj_in, 16 * i + 16)
                pool.tensor_scalar(adjs[:, :, :], adjs[:, :, :], 2.0 * SCALE, None, ALU.mult).then_inc(adj_scaled, 1)

            def x_plus_bo(i):
                wait_apart(pool, x_in, 16 * i + 16)
                pool.tensor_tensor(x2[:, bass.ds(i * BJ, BJ), :], xin[:, :, :],
                                   boB[:, :].unsqueeze(1).to_broadcast([P, BJ, D]), ALU.add).then_inc(xbo_done, 1)

            def sub_max(i):
                for r in range(R):
                    wait_apart(pool, mx_done, R * i + r + 1)
                    v = sm[:, r, :].rearrange("p (a k) -> p a k", k=S)
                    pool.tensor_tensor(v, v, mx[:, r, :].unsqueeze(2).to_broadcast([P, 8, S]), ALU.subtract).then_inc(sub_done, 1)

            def normalise(i):
                for r in range(R):
                    wait_apart(pool, rsum_done, R * i + r + 1)
                    v = sm[:, r, :].rearrange("p (a k) -> p a k", k=S)
                    pool.tensor_tensor(v, v, sums[:, r, :].unsqueeze(2).to_broadcast([P, 8, S]), ALU.mult).then_inc(prob_done, 1)

            def carry(i):
                if not isinstance(i, int) or i > 0:
                    wait_apart(pool, scattered, 16 * BJ * K * i)
                pool.tensor_copy(row[:, :, :, D:D + 1].bitcast(I32).rearrange("p j k o -> p j (k o)"),
                                 ids[:, bass.ds(i * BJ, BJ), :]).then_inc(ids_done, 1)

            def scatter(i):
                wait_apart(pool, ids_done, i + 1)
                wait_apart(pool, dst_done, i + 1)
                wait_apart(pool, row_done, i + 1)
                wait_apart(pool, row2_done, i + 1)
                for j in range(BJ):
                    for k in range(K):
                        n = j * K + k
                        pool.indirect_dma_start(rows, bass.IndirectOffsetOnAxis(dst[:, n:n + 1], 0), row[:, j, k, :], None,
                                                bounds_check=PAD0 - 1, oob_is_err=False).then_inc(scattered, 16)

            def body(i, first=False, more=True, last=False):
                sub_max(i)
                if not last:
                    wait_apart(pool, masked, R * i + R)
                    scale_mask(i + 1)
                if not first:
                    carry(i - 1)
                normalise(i)
                if not first:
                    scatter(i - 1)
                if more:
                    x_plus_bo(i + 2)

            pool.wait_ge(consts, NCONST)
            scale_mask(0)
            pool.wait_ge(su_act, SU_BO)
            x_plus_bo(0)
            x_plus_bo(1)
            body(0, first=True)
            with pool.Fori(1, NBLK - 2) as i:
                body(i)
            body(NBLK - 2, more=False)
            body(NBLK - 1, more=False, last=True)
            carry(NBLK - 1)
            scatter(NBLK - 1)

            def keep_places(n, nb, b):
                wait_apart(pool, g_in[b], 16 * nb + 16)
                pool.tensor_copy(places_kept[:, bass.ds(n, 1), :].rearrange("p o s -> p (o s)"),
                                 gin[b][:, :, D:D + 1].bitcast(I32).rearrange("p s o -> p (s o)")).then_inc(kept, 1)

            def finish(n, b):
                e = pool.value_load(tab[0:1, 1, bass.ds(n, 1)], min_val=0, max_val=E - 1)
                wait_apart(pool, kept, n + 1)
                wait_apart(pool, ys_done, n + 1)
                pool.tensor_copy(yidx[b][:, :], places_kept[:, bass.ds(n, 1), :].rearrange("p o s -> p (o s)")).then_inc(yidx_done, 1)
                pool.tensor_tensor(yout[b], yout[b], beB[:, bass.ds(e, 1), :].to_broadcast([P, GS, D]), ALU.add).then_inc(yo_done, 1)
                wait_apart(pool, yo_done, n + 1)
                wait_apart(pool, yidx_done, n + 1)
                for s in range(GS):
                    pool.indirect_dma_start(results, bass.IndirectOffsetOnAxis(yidx[b][:, s:s + 1], 0), yout[b][:, s, :], None,
                                            bounds_check=K * T + 2 * E * GT - 1, oob_is_err=False).then_inc(y_out[b], 16)

            wait_apart(pool, scattered, 16 * BJ * K * NBLK)
            pool.wait_ge(tab_done, 1)
            for n in range(4):
                keep_places(n, n // 2, n % 2)
            keep_places(4, 2, 0)
            finish(0, 0)
            with pool.Fori(0, (NG - 5) // 2) as m:
                keep_places(2 * m + 5, m + 2, 1)
                finish(2 * m + 1, 1)
                keep_places(2 * m + 6, m + 3, 0)
                finish(2 * m + 2, 0)
            for n in range(NG - 4, NG):
                finish(n, n % 2)
            for b in range(2):
                pool.wait_ge(y_out[b], 16 * GS * ((NG + 1 - b) // 2))

        @block.vector
        def _(dve):
            dve.memset(vb[:, :, :, :, :].rearrange("p a b c d -> p (a b c d)"), 0.0).then_inc(dconst, 1)
            dve.memset(onesf[:, :], 1.0).then_inc(dconst, 1)
            dve.memset(one8[:, :], 1.0).then_inc(dconst, 1)
            dve.memset(run[:, :], 0.0).then_inc(dconst, 1)
            dve.memset(runb[:, :], 0.0).then_inc(dconst, 1)
            dve.wait_ge(setup_in, 16 * SETUP_LOADS)
            wo_nat = pTf[:, 1536:2048].rearrange("p (f hh c r d) -> p f c r hh d", f=KC, hh=2, c=KC, r=2)
            for f in range(KC):
                for c in range(KC):
                    o = smf[:, (f * KC + c) * P:(f * KC + c + 1) * P].rearrange("p (r hh d) -> p r hh d", r=2, hh=2)
                    ins = dve.tensor_copy(o, wo_nat[:, f, c])
            ins.then_inc(wo_perm, 1)
            dve.wait_ge(su_act, 1)
            for c in range(KC):
                ins = dve.tensor_copy(bvb[:, c, :], cols[:, 20 + c:21 + c].to_broadcast([P, P]))
            ins.then_inc(bvb_done, 1)

            LN = 6

            def layernorm(n, src, which, s, out_, done):
                c = 0
                for j in range(BJ):
                    ins = dve.bn_stats(st[:, j, :], src(j))
                ins.then_inc(s, 1)
                wait_apart(dve, s, LN * n + 1)
                for j in range(BJ):
                    ins = dve.bn_aggr(mv[:, j, :], st[:, j, :])
                ins.then_inc(s, 1)
                dve.wait_ge(s, LN * n + 2)
                dve.tensor_scalar(var[:, :], mv[:, :, 1], EPS, None, ALU.add).then_inc(var_done, 1)
                dve.wait_ge(rs0_done, which(n))
                dve.tensor_tensor(tmp[:, :], var[:, :], rs0[:, :], ALU.mult).then_inc(s, 1)
                dve.wait_ge(s, LN * n + 3)
                dve.tensor_tensor(tmp[:, :], tmp[:, :], rs0[:, :], ALU.mult).then_inc(s, 1)
                dve.wait_ge(s, LN * n + 4)
                dve.tensor_scalar(tmp[:, :], tmp[:, :], -0.5, 1.5, ALU.mult, ALU.add).then_inc(s, 1)
                dve.wait_ge(s, LN * n + 5)
                dve.tensor_tensor(rstd[:, :], tmp[:, :], rs0[:, :], ALU.mult).then_inc(s, 1)
                dve.wait_ge(s, LN * n + 6)
                for j in range(BJ):
                    ins = dve.tensor_scalar(out_(j), src(j), mv[:, j, 0:1], rstd[:, j:j + 1], ALU.subtract, ALU.mult)
                ins.then_inc(done, 1)

            def ln1(i):
                if not isinstance(i, int) or i > 0:
                    dve.wait_ge(xT_ps, KC * i)
                wait_apart(dve, x_in, 16 * i + 16)
                layernorm(i, lambda j: xin[:, j, :], lambda n: LN1_AT(n), ln1_s, lambda j: xn[:, j, :], xn_done)

            def LN1_AT(n):
                return n + 1 if isinstance(n, int) and n < 2 else 2 * n - 1

            def LN2_AT(n):
                return NBLK + n + 1 if isinstance(n, int) and n >= NBLK - 2 else 2 * n + 4

            def ln2(i):
                if not isinstance(i, int) or i > 0:
                    wait_apart(dve, scattered, 16 * BJ * K * i)
                layernorm(i, lambda j: x2[:, bass.ds(i * BJ + j, 1), :].rearrange("p o d -> p (o d)"), lambda n: LN2_AT(n),
                          ln2_s, lambda j: row[:, j, 0, 0:D], row_done)

            def mask_and_max(i):
                dve.wait_ge(adj_scaled, i + 1)
                dve.wait_ge(s_ps, i + 1)
                for r in range(R):
                    a = adjs[:, :, :].unsqueeze(2).to_broadcast([P, BJ, 2, S])
                    dve.tensor_tensor(sm[:, r, :].rearrange("p (j h k) -> p j h k", j=BJ, h=2),
                                      SBK[r][:, :].rearrange("p (j h k) -> p j h k", j=BJ, h=2), a, ALU.mult).then_inc(masked, 1)
                for r in range(R):
                    dve.wait_ge(masked, R * i + r + 1)
                    dve.tensor_reduce(mx[:, r, :], sm[:, r, :].rearrange("p (a k) -> p a k", k=S), AX_X, ALU.max).then_inc(mx_done, 1)

            def prob_sums(i):
                for r in range(R):
                    dve.wait_ge(exp_done, R * i + r + 1)
                    dve.tensor_reduce(sums[:, r, :], sm[:, r, :].rearrange("p (a k) -> p a k", k=S), AX_X, ALU.add).then_inc(sum_s, 1)
                    dve.wait_ge(sum_s, R * i + r + 1)
                    dve.reciprocal(sums[:, r, :], sums[:, r, :]).then_inc(rsum_done, 1)

            def route_a(i):
                n = 0
                dve.wait_ge(lg_ps, i + 1)
                dve.tensor_copy(lg[:, :, :].rearrange("p j e -> p (j e)"), RB[:, 0:BJ * E]).then_inc(rt, 1)
                wait_apart(dve, rt, RT * i + 1)
                for j in range(BJ):
                    ins = dve.max(top[:, j, :], lg[:, j, :])
                ins.then_inc(rt, 1)
                wait_apart(dve, rt, RT * i + 2)
                for j in range(BJ):
                    ins = dve.max_index(topi[:, j, :], top[:, j, :], lg[:, j, :])
                ins.then_inc(rt, 1)
                dve.tensor_tensor(gd[:, :], top[:, :, 1], top[:, :, 0], ALU.subtract).then_inc(gd_done, 1)
                dve.wait_ge(rt, RT * i + 3)
                dve.tensor_copy(e12[:, :, :], topi[:, :, 0:K]).then_inc(rt, 1)
                dve.wait_ge(rt, RT * i + 4)
                dve.tensor_tensor(hot[:, :, :, :].rearrange("p j k e -> p (j k) e"),
                                  iota_e[:, :].unsqueeze(1).to_broadcast([P, BJ * K, E]),
                                  e12[:, :, :].rearrange("p j k -> p (j k)").unsqueeze(2).to_broadcast([P, BJ * K, E]),
                                  ALU.is_equal).then_inc(rt, 1)
                dve.wait_ge(rt, RT * i + 5)
                dve.tensor_tensor(both[:, :, :], hot[:, :, 0, :], hot[:, :, 1, :], ALU.add).then_inc(both_done, 1)

            def route_b(i):
                dve.wait_ge(place_ps, i + 1)
                dve.tensor_tensor(place[:, :, :], RB[:, 64:64 + BJ * E].rearrange("p (j e) -> p j e", j=BJ),
                                  base_e[:, :].unsqueeze(1).to_broadcast([P, BJ, E]), ALU.add).then_inc(rt, 1)
                dve.tensor_reduce(blk[:, :], both[:, :, :].rearrange("p j e -> p e j"), AX_X, ALU.add).then_inc(rt, 1)
                dve.wait_ge(rt, RT * i + 6)
                dve.tensor_tensor(sel[:, :, :, :], hot[:, :, :, :], place[:, :, :].unsqueeze(2).to_broadcast([P, BJ, K, E]),
                                  ALU.mult).then_inc(rt, 1)
                dve.wait_ge(rt, RT * i + 7)
                dve.tensor_tensor(run[:, :], run[:, :], blk[:, :], ALU.add).then_inc(rt, 1)
                dve.wait_ge(rt, RT * i + 8)
                dve.tensor_reduce(dstf[:, :], sel[:, :, :, :].rearrange("p j k e -> p (j k) e"), AX_X, ALU.add).then_inc(rt, 1)
                dve.wait_ge(rt, RT * i + 9)
                dve.tensor_copy(runb[:, :], run[:, :]).then_inc(rt, 1)
                dve.wait_ge(rt, RT * i + 10)
                if not isinstance(i, int) or i > 0:
                    dve.wait_ge(scattered, 16 * BJ * K * i)
                dve.tensor_copy(dst[:, :], dstf[:, :]).then_inc(dst_done, 1)
                dve.wait_ge(gx_done, i + 1)
                dve.tensor_scalar(gs[:, :], gx[:, :], 1.0, None, ALU.add).then_inc(rt, 1)
                dve.wait_ge(rt, RT * i + 12)
                dve.reciprocal(gs[:, :], gs[:, :]).then_inc(rt, 1)
                dve.wait_ge(rt, RT * i + 13)
                dve.tensor_copy(gates[:, bass.ds(i * BJ, BJ), 0:1].rearrange("p j o -> p (j o)"), gs[:, :]).then_inc(rt, 1)
                dve.tensor_tensor(gates[:, bass.ds(i * BJ, BJ), 1:2].rearrange("p j o -> p (j o)"), gx[:, :], gs[:, :], ALU.mult).then_inc(rt, 1)

            def residual(i):
                for jj in range(2):
                    dve.wait_ge(xbo_done, i + 1)
                    dve.wait_ge(o_ps, 2 * i + jj + 1)
                    v = x2[:, bass.ds(i * BJ + 2 * jj, 2), :].rearrange("p j d -> p (j d)")
                    ins = dve.tensor_tensor(v, (W0, W1b)[jj][:, :], v, ALU.add)
                    ins.then_inc(res_done, 1)
                wait_apart(dve, res_done, 2 * i + 2)

            def body(i, first=False, more=True):
                mask_and_max(i)
                prob_sums(i)
                if more:
                    ln1(i + 2)
                if not first:
                    route_a(i - 1)
                    route_b(i - 1)
                residual(i)
                ln2(i)

            ln1(0)
            ln1(1)
            body(0, first=True)
            with dve.Fori(1, NBLK - 2) as i:
                body(i)
            body(NBLK - 2, more=False)
            body(NBLK - 1, more=False)
            route_a(NBLK - 1)
            route_b(NBLK - 1)

            tn = [0]

            def t(ins):
                tn[0] += 1
                ins.then_inc(tb, 1)
                dve.wait_ge(tb, tn[0])

            dve.wait_ge(cnt_ps, 1)
            t(dve.tensor_copy(cnt[:, :], RB[:, 0:E]))
            t(dve.tensor_scalar(ngf[:, :], cnt[:, :], float(GT - 1), None, ALU.add))
            t(dve.tensor_copy(ngi[:, :], ngf[:, :]))
            t(dve.tensor_scalar(ngi[:, :], ngi[:, :], GT.bit_length() - 1, None, ALU.logical_shift_right))
            t(dve.tensor_copy(ngf[:, :], ngi[:, :]))
            t(dve.tensor_tensor_scan(cum[:, :], one8[:, :], ngf[:, :], 0.0, ALU.mult, ALU.add))
            t(dve.tensor_tensor(padf[:, :], cnt[0:1, :], base_e[0:1, :], ALU.add))
            t(dve.tensor_copy(padi[:, :], padf[:, :]))
            t(dve.tensor_tensor(ge[:, :, :], iota_g[:, :].unsqueeze(2).to_broadcast([1, NG, E]),
                                cum[0:1, :].unsqueeze(1).to_broadcast([1, NG, E]), ALU.is_ge))
            t(dve.tensor_tensor(gg[:, :, :], ge[:, :, :], ngf[0:1, :].unsqueeze(1).to_broadcast([1, NG, E]), ALU.mult))
            t(dve.tensor_reduce(gexp[:, :], ge[:, :, :], AX_X, ALU.add))
            t(dve.tensor_reduce(gprev[:, :], gg[:, :, :], AX_X, ALU.add))
            t(dve.tensor_scalar(tabf[:, 0, :], gexp[:, :], float(CAPG), None, ALU.mult))
            t(dve.tensor_tensor(tabf[:, 0, :], tabf[:, 0, :], gprev[:, :], ALU.subtract))
            t(dve.tensor_tensor(tabf[:, 0, :], tabf[:, 0, :], iota_g[:, :], ALU.add))
            t(dve.tensor_scalar(tabf[:, 0, :], tabf[:, 0, :], float(GT), None, ALU.mult))
            t(dve.tensor_scalar(tabf[:, 1, :], gexp[:, :], float(E - 1), None, ALU.min))
            dve.tensor_copy(tab[:, :, :], tabf[:, :, :]).then_inc(tab_done, 1)

            def group(n, b):
                e = dve.value_load(tab[0:1, 1, bass.ds(n, 1)], min_val=0, max_val=E - 1)
                if not isinstance(n, int) or n > 1:
                    dve.wait_ge(ys_done, n - 1)
                dve.wait_ge(y_ps, n + 1)
                dve.tensor_tensor(ybuf[b], YB[b][:, :].rearrange("p (s d) -> p s d", s=GS),
                                  b2B[:, bass.ds(e, 1), :].to_broadcast([P, GS, D]), ALU.add).then_inc(y_read, 1)
                wait_apart(dve, y_read, n + 1)
                for q in range(GS):
                    ins = dve.bn_stats(yst[:, q, :], ybuf[b][:, q, :])
                ins.then_inc(yb, 1)
                wait_apart(dve, yb, YS * n + 1)
                for q in range(GS):
                    ins = dve.bn_aggr(ymv[:, q, :], yst[:, q, :])
                ins.then_inc(yb, 1)
                dve.wait_ge(yb, YS * n + 2)
                dve.tensor_scalar(yva[:, :], ymv[:, :, 1], EPS, None, ALU.add).then_inc(yvar, 1)
                for q in range(GS):
                    dve.scalar_tensor_tensor(ybuf[b][:, q, :], ybuf[b][:, q, :], ymv[:, q, 0:1],
                                             gaB[:, bass.ds(e, 1), :].rearrange("p o d -> p (o d)"), ALU.subtract, ALU.mult)
                dve.wait_ge(yrs0, n + 1)
                dve.tensor_tensor(ytm[:, :], yva[:, :], yr0[:, :], ALU.mult).then_inc(yb, 1)
                dve.wait_ge(yb, YS * n + 3)
                dve.tensor_tensor(ytm[:, :], ytm[:, :], yr0[:, :], ALU.mult).then_inc(yb, 1)
                dve.wait_ge(yb, YS * n + 4)
                dve.tensor_scalar(ytm[:, :], ytm[:, :], -0.5, 1.5, ALU.mult, ALU.add).then_inc(yb, 1)
                dve.wait_ge(yb, YS * n + 5)
                dve.tensor_tensor(yrs[b][:, :], ytm[:, :], yr0[:, :], ALU.mult).then_inc(yrs_done, 1)

            YS = 5
            dve.wait_ge(tab_done, 1)
            dve.wait_ge(experts_in, 16 * EXPERT_LOADS)
            for n in range(3):
                group(n, n % 2)
            with dve.Fori(0, (NG - 3) // 2) as m:
                group(2 * m + 3, 1)
                group(2 * m + 4, 0)

            def combine(i, nb, b):
                dve.wait_ge(r_in[b], 16 * K * (nb + 1))
                for k in range(K):
                    for j in range(BJ):
                        v = x2[:, bass.ds(i * BJ + j, 1), :].rearrange("p o d -> p (o d)")
                        g = gates[:, bass.ds(i * BJ + j, 1), k:k + 1].rearrange("p o k -> p (o k)")
                        ins = dve.scalar_tensor_tensor(v, rbuf[b][k][:, j, :], g, v, ALU.mult, ALU.add)
                    if k == 0:
                        ins.then_inc(f_s, 1)
                        dve.wait_ge(f_s, i + 1)
                ins.then_inc(f_done, 1)

            with dve.Fori(0, NBLK // NR) as m:
                for b in range(NR):
                    combine(NR * m + b, m, b)

        @block.scalar
        def _(act):
            nc.scalar.preload_act_table_set("natural_log_exp_and_others")

            def copy(o, i_, sem_):
                act.activation(o, i_, ACT.Copy).then_inc(sem_, 1)

            act.wait_ge(su_pe, 1)
            copy(cols[:, :], W0[:, 0:22], su_act)
            for n, w in enumerate((wqT, wkT, wvT, woT)):
                act.wait_ge(su_pe, n + 2)
                copy(w[:, :, :].rearrange("p c f -> p (c f)"), SBK[n][:, :], su_act)
            act.wait_ge(su_pe, 6)
            copy(boB[:, :], W1b[:, 0:D], su_act)

            def rsqrt_start(n):
                act.wait_ge(var_done, n + 1)
                act.activation(lnv[:, :], var[:, :], ACT.Ln).then_inc(lnv_done, 1)
                act.wait_ge(lnv_done, n + 1)
                act.activation(rs0[:, :], lnv[:, :], ACT.Exp, scale=-0.5).then_inc(rs0_done, 1)

            def x_copies(i):
                for c in range(KC):
                    act.wait_ge(xT_ps, KC * i + c + 1)
                    copy(xT[:, c, :], (W2b, W0)[c][:, :], xT_done)

            def qk_copy(i, m):
                act.wait_ge(qk_ps, 4 * i + m + 1)
                act.activation((qT, kT)[m // 2][:, m % 2, :], (W1b, W2b, W0, W1b)[m][:, :], ACT.Identity,
                               bias=cols[:, 16 + m:17 + m]).then_inc(qk_done, 1)

            def exps(i, r):
                act.wait_ge(sub_done, R * i + r + 1)
                act.activation(sm[:, r, :], sm[:, r, :], ACT.Exp).then_inc(exp_done, 1)

            def v_copies(i):
                for jj in range(2):
                    act.wait_ge(v_ps, 2 * i + jj + 1)
                    for g in range(GPT):
                        for hh in range(2):
                            src = (W1b, W2b)[jj][S * g:S * g + S, :].rearrange("p (j h r d) -> p j h r d", j=2, h=2, r=R)[:, :, hh]
                            o = vb[S * hh:S * hh + S, :, :, hh, :].rearrange("p (j g) r d -> p j g r d", g=GPT)[:, 2 * jj:2 * jj + 2, g]
                            ins = act.activation(o, src, ACT.Copy)
                    ins.then_inc(v_done, 1)

            def h_copies(i):
                for c in range(KC):
                    act.wait_ge(h_ps, KC * i + c + 1)
                    copy(hT2[:, c, :], (W0, W1b)[c][:, :], h_done)

            def body(i, first=False, more=True, last=False):
                if not last:
                    x_copies(i + 1)
                for r in range(R):
                    if not last:
                        if r == 0:
                            act.wait_ge(s_ps, i + 1)
                        qk_copy(i + 1, r)
                    exps(i, r)
                if not first:
                    h_copies(i - 1)
                for r in range(R):
                    act.wait_ge(pT_ps, R * i + r + 1)
                    copy(pT[:, r, :], SBK[r][:, :], pT_done)
                if more:
                    rsqrt_start(2 * i + 2)
                if not first:
                    act.wait_ge(gd_done, i)
                    act.activation(gx[:, :], gd[:, :], ACT.Exp).then_inc(gx_done, 1)
                for c in range(KC):
                    act.wait_ge(c_ps, KC * i + c + 1)
                    copy(cT[:, c, :], (W2b, W0)[c][:, :], c_done)
                if not last:
                    v_copies(i + 1)
                rsqrt_start(2 * i + 3 if more else NBLK + i)
                act.wait_ge(row_done, i + 1)
                act.activation(row[:, :, 1, 0:D], row[:, :, 0, 0:D], ACT.Copy).then_inc(row2_done, 1)

            rsqrt_start(0)
            act.wait_ge(dconst, 5)
            x_copies(0)
            rsqrt_start(1)
            for m in range(4):
                qk_copy(0, m)
            v_copies(0)
            body(0, first=True)
            with act.Fori(1, NBLK - 2) as i:
                body(i)
            body(NBLK - 2, more=False)
            body(NBLK - 1, more=False, last=True)
            h_copies(NBLK - 1)
            act.wait_ge(gd_done, NBLK)
            act.activation(gx[:, :], gd[:, :], ACT.Exp).then_inc(gx_done, 1)

            def expert_of(n):
                return act.value_load(tab[0:1, 1, bass.ds(n, 1)], min_val=0, max_val=E - 1)

            def weights(e, layer, b):
                act.activation(wc[layer][b], we[:, bass.ds(e, 1), 2 * layer:2 * layer + 2, :].rearrange("p o k f -> p (o k) f"),
                               ACT.Copy).then_inc(w_cur[layer], 1)

            def g_copy(n, b):
                act.wait_ge(gT_ps, n + 1)
                act.activation(gT[b], GTB[b][:, :].rearrange("p (k t) -> p k t", k=KC), ACT.Copy).then_inc(gT_done, 1)

            def hidden(n, e, b):
                act.wait_ge(m_ps, n + 1)
                for c in range(2):
                    act.activation(mT[b][:, c, :], MB[b][:, c * GT:(c + 1) * GT], ACT.Relu,
                                   bias=cols[:, bass.ds(e * 2 + c, 1)]).then_inc(m_done, 1)

            def y_rsqrt(n):
                act.wait_ge(yvar, n + 1)
                act.activation(yln[:, :], yva[:, :], ACT.Ln).then_inc(ylnv, 1)
                act.wait_ge(ylnv, n + 1)
                act.activation(yr0[:, :], yln[:, :], ACT.Exp, scale=-0.5).then_inc(yrs0, 1)

            def y_scale(n, nb, b):
                act.wait_ge(yrs_done, n + 1)
                if not isinstance(nb, int) or nb > 0:
                    act.wait_ge(y_out[b], 16 * GS * nb)
                for q in range(GS):
                    ins = act.activation(yout[b][:, q, :], ybuf[b][:, q, :], ACT.Copy, scale=yrs[b][:, q:q + 1])
                ins.then_inc(ys_done, 1)

            def step(n, nb, b):
                if not isinstance(n, int) or n < NG - 2:
                    act.wait_ge(m_ps, n + 1)
                    g_copy(n + 2, b)
                if not isinstance(n, int) or n > 1:
                    y_scale(n - 2, nb, b)
                if not isinstance(n, int) or n < NG - 2:
                    weights(expert_of(n + 2), 0, b)
                if not isinstance(n, int) or n < NG - 1:
                    e = expert_of(n + 1)
                    if not isinstance(n, int) or n > 0:
                        act.wait_ge(y_ps, n)
                    weights(e, 1, 1 - b)
                    hidden(n + 1, e, 1 - b)
                if not isinstance(n, int) or n > 0:
                    y_rsqrt(n - 1)

            act.wait_ge(tab_done, 1)
            act.wait_ge(experts_in, 16 * EXPERT_LOADS)
            e0 = expert_of(0)
            weights(e0, 0, 0)
            weights(expert_of(1), 0, 1)
            weights(e0, 1, 0)
            g_copy(0, 0)
            g_copy(1, 1)
            hidden(0, e0, 0)
            for n in range(4):
                step(n, 0, n % 2)
            step(4, 1, 0)
            with act.Fori(0, (NG - 7) // 2) as m:
                step(2 * m + 5, m + 1, 1)
                step(2 * m + 6, m + 2, 0)
            step(NG - 2, (NG - 4) // 2, 1)
            step(NG - 1, (NG - 3) // 2, 0)
            y_scale(NG - 2, (NG - 2) // 2, 1)
            y_rsqrt(NG - 1)
            y_scale(NG - 1, (NG - 1) // 2, 0)

            with act.Fori(0, NBLK) as i:
                act.wait_ge(f_done, i + 1)
                act.dma_start(outt[bass.ds(i, 1)].rearrange("o p j d -> (o p) j d"),
                              x2[:, bass.ds(i * BJ, BJ), :]).then_inc(o_out, 16)
            act.wait_ge(o_out, 16 * NBLK)

        @block.tensor
        def _(pe):
            pe.wait_ge(consts, NCONST)
            pe.wait_ge(setup_in, 16 * SETUP_LOADS)
            pe.transpose(W0[:, 0:22], small_rows[:, :], ident[0:22, 0:22]).then_inc(su_pe, 1)
            for n in range(4):
                if n == 3:
                    pe.wait_ge(wo_perm, 1)
                nat = (pTf[:, 512 * n:512 * n + 512] if n < 3 else smf[:, 0:512]).rearrange("p (f e) -> p f e", f=KC)
                for c in range(KC):
                    for f in range(KC):
                        mm = pe.transpose(SBK[n][:, c * D + f * P:c * D + (f + 1) * P], nat[:, f, c * P:(c + 1) * P], ident[:, :])
                mm.then_inc(su_pe, 1)
            pe.wait_ge(bvb_done, 1)
            pe.wait_ge(su_act, 5)
            pe.wait_ge(dconst, 5)
            for c in range(KC):
                pe.matmul(W1b[:, 0:D], bvb[:, c, :], woT[:, c, :], start=(c == 0), stop=False)
            pe.matmul(W1b[:, 0:D], onesf[:, :], boB[0:1, :], start=False, stop=True).then_inc(su_pe, 1)
            pe.wait_ge(su_act, 6)

            def x_transposes(i):
                pe.wait_ge(xn_done, i + 1)
                for c in range(KC):
                    if not isinstance(i, int) or i > 0:
                        if c == 0:
                            pe.wait_ge(v_done, 2 * i)
                        elif isinstance(i, int) and i == 1:
                            pe.wait_ge(qk_done, 3)
                        else:
                            pe.wait_ge(res_done, 2 * (i - 2) + 1)
                    for j in range(BJ):
                        mm = pe.transpose((W2b, W0)[c][:, j * P:(j + 1) * P], xn[:, j, c * P:(c + 1) * P], ident[:, :])
                    mm.then_inc(xT_ps, 1)

            def qk(i):
                pe.wait_ge(xT_done, KC * i + KC)
                if not isinstance(i, int) or i > 1:
                    pe.wait_ge(res_done, 2 * (i - 1))
                for m in range(4):
                    if m == 3:
                        pe.wait_ge(qk_done, 4 * i + 1)
                    for c in range(KC):
                        mm = pe.matmul((W1b, W2b, W0, W1b)[m][:, :], (wqT, wkT)[m // 2][:, c, (m % 2) * P:(m % 2 + 1) * P],
                                       xT[:, c, :], start=(c == 0), stop=(c == KC - 1))
                    mm.then_inc(qk_ps, 1)

            def v(i):
                for jj in range(2):
                    if jj == 0:
                        pe.wait_ge(qk_done, 4 * i + 4)
                        if not isinstance(i, int) or i > 1:
                            pe.wait_ge(h_done, KC * (i - 1))
                    elif not isinstance(i, int) or i > 0:
                        pe.wait_ge(c_done, KC * (i - 1) + 1)
                    for j in range(2):
                        t0 = (2 * jj + j) * P
                        for c in range(KC):
                            mm = pe.matmul((W1b, W2b)[jj][:, j * D:(j + 1) * D], xT[:, c, t0:t0 + P], wvT[:, c, :],
                                           start=(c == 0), stop=(c == KC - 1))
                    mm.then_inc(v_ps, 1)

            def scores(i):
                pe.wait_ge(qk_done, 4 * i + 4)
                if not isinstance(i, int) or i > 0:
                    pe.wait_ge(pT_done, R * i)
                for j in range(BJ):
                    for g in range(GPT):
                        t0 = j * P + g * S
                        for hh in range(2):
                            for r in range(R):
                                mm = pe.matmul(SBK[r][S * g:S * g + S, (2 * j + hh) * S:(2 * j + hh + 1) * S],
                                               qT[Dh * r:Dh * r + Dh, hh, t0:t0 + S], kT[Dh * r:Dh * r + Dh, hh, t0:t0 + S],
                                               start=True, stop=True)
                mm.then_inc(s_ps, 1)

            def row_transposes(i, last=False):
                pe.wait_ge(row_done, i + 1)
                for c in range(KC):
                    if not last:
                        pe.wait_ge(qk_done, 4 * (i + 2) + 3 + c)
                    for j in range(BJ):
                        mm = pe.transpose((W0, W1b)[c][:, j * P:(j + 1) * P], row[:, j, 0, c * P:(c + 1) * P], ident[:, :])
                    mm.then_inc(h_ps, 1)

            def logits(i):
                pe.wait_ge(h_done, KC * i + KC)
                for j in range(BJ):
                    for c in range(KC):
                        mm = pe.matmul(RB[:, j * E:(j + 1) * E], hT2[:, c, j * P:(j + 1) * P], wg[:, c, :],
                                       start=(c == 0), stop=(c == KC - 1))
                mm.then_inc(lg_ps, 1)

            def places(i):
                pe.wait_ge(both_done, i + 1)
                o = RB[:, 64:64 + BJ * E]
                pe.matmul(o, upper[:, :], both[:, :, :].rearrange("p j e -> p (j e)"), start=True, stop=False, skip_group_check=True)
                for j in range(BJ - 1):
                    w = BJ - 1 - j
                    pe.matmul(RB[:, 64 + (j + 1) * E:64 + BJ * E].rearrange("p (j e) -> p j e", j=w), ones[:, :],
                              both[:, j, :].unsqueeze(1).to_broadcast([P, w, E]), start=False, stop=False, skip_group_check=True)
                pe.matmul(o.rearrange("p (j e) -> p j e", j=BJ), ones[:, :], runb[:, :].unsqueeze(1).to_broadcast([P, BJ, E]),
                          start=False, stop=True, skip_group_check=True).then_inc(place_ps, 1)

            def prob_transposes(i):
                for r in range(R):
                    pe.wait_ge(prob_done, R * i + r + 1)
                    for j in range(BJ):
                        mm = pe.transpose(SBK[r][:, j * P:(j + 1) * P], sm[:, r, j * P:(j + 1) * P], ident[:, :])
                    mm.then_inc(pT_ps, 1)

            def context(i, c, first, last):
                pe.wait_ge(pT_done, R * i + 2 * c + 2)
                if c == 0:
                    pe.wait_ge(v_done, 2 * i + 2)
                    if not last:
                        pe.wait_ge(qk_done, 4 * i + 4 + 2)
                elif first:
                    pe.wait_ge(qk_done, 4 * i + 4 + 3)
                else:
                    pe.wait_ge(h_done, KC * (i - 1) + 1)
                for j in range(BJ):
                    for g in range(GPT):
                        t0 = j * P + g * S
                        for r2 in range(2):
                            mm = pe.matmul((W2b, W0)[c][S * r2:S * r2 + S, t0:t0 + S],
                                           vb[:, 2 * j + g, 2 * c + r2, :, :].rearrange("p h d -> p (h d)"),
                                           pT[:, 2 * c + r2, t0:t0 + S], start=True, stop=True)
                mm.then_inc(c_ps, 1)

            def output(i, last):
                pe.wait_ge(c_done, KC * i + KC)
                for jj in range(2):
                    if jj == 1:
                        if last:
                            pe.wait_ge(h_done, KC * i)
                        else:
                            pe.wait_ge(v_done, 2 * i + 3)
                    for j in range(2):
                        t0 = (2 * jj + j) * P
                        for c in range(KC):
                            mm = pe.matmul((W0, W1b)[jj][:, j * D:(j + 1) * D], cT[:, c, t0:t0 + P], woT[:, c, :],
                                           start=(c == 0), stop=(c == KC - 1))
                    mm.then_inc(o_ps, 1)

            def body(i, first, last):
                if not last:
                    x_transposes(i + 1)
                scores(i)
                if not last:
                    qk(i + 1)
                if not first:
                    row_transposes(i - 1, last)
                prob_transposes(i)
                if not first:
                    logits(i - 1)
                context(i, 0, first, last)
                context(i, 1, first, last)
                if not first:
                    places(i - 1)
                if not last:
                    v(i + 1)
                output(i, last)

            x_transposes(0)
            qk(0)
            v(0)
            body(0, True, False)
            with pe.Fori(1, NBLK - 1) as i:
                body(i, False, False)
            body(NBLK - 1, False, True)
            row_transposes(NBLK - 1, last=True)
            logits(NBLK - 1)
            places(NBLK - 1)
            pe.wait_ge(rt, RT * NBLK)
            pe.matmul(RB[:, 0:E], ones[:, :], runb[:, :], start=True, stop=True).then_inc(cnt_ps, 1)

            def late(n, first):
                return not isinstance(n, int) or n >= first

            def group_transposes(n, nb, b):
                pe.wait_ge(g_in[b], 16 * (nb + 1))
                if late(n, 2):
                    pe.wait_ge(gT_done, n - 1)
                for c in range(KC):
                    for s in range(GS):
                        mm = pe.transpose(GTB[b][:, c * GT + s * P:c * GT + (s + 1) * P], gin[b][:, s, c * P:(c + 1) * P], ident[:, :])
                mm.then_inc(gT_ps, 1)

            def layer1(n, b):
                pe.wait_ge(gT_done, n + 1)
                pe.wait_ge(w_cur[0], n + 1)
                if late(n, 2):
                    pe.wait_ge(m_done, 2 * (n - 1))
                for m in range(2):
                    for c in range(KC):
                        mm = pe.matmul(MB[b][:, m * GT:(m + 1) * GT], wc[0][b][:, c, m * P:(m + 1) * P], gT[b][:, c, :],
                                       start=(c == 0), stop=(c == KC - 1))
                mm.then_inc(m_ps, 1)

            def layer2(n, b):
                pe.wait_ge(m_done, 2 * n + 2)
                pe.wait_ge(w_cur[1], n + 1)
                if late(n, 2):
                    pe.wait_ge(y_read, n - 1)
                for s in range(GS):
                    for c in range(2):
                        mm = pe.matmul(YB[b][:, s * D:(s + 1) * D], mT[b][:, c, s * P:(s + 1) * P], wc[1][b][:, c, :],
                                       start=(c == 0), stop=(c == 1))
                mm.then_inc(y_ps, 1)

            def step(n, nb, b):
                if not isinstance(n, int) or n < NG - 2:
                    group_transposes(n + 2, nb, b)
                if not isinstance(n, int) or n < NG - 1:
                    layer1(n + 1, 1 - b)
                layer2(n, b)

            group_transposes(0, 0, 0)
            group_transposes(1, 0, 1)
            layer1(0, 0)
            for n in range(3):
                step(n, n // 2 + 1, n % 2)
            with pe.Fori(0, (NG - 5) // 2) as m:
                step(2 * m + 3, m + 2, 1)
                step(2 * m + 4, m + 3, 0)
            step(NG - 2, 0, 1)
            step(NG - 1, 0, 0)


_INS = ["x", "adj", "L0_gnn_Wq", "L0_gnn_bq", "L0_gnn_Wk", "L0_gnn_bk", "L0_gnn_Wv", "L0_gnn_bv", "L0_gnn_Wo", "L0_gnn_bo",
        "L0_ffn_Wg", "L0_ffn_W1", "L0_ffn_b1", "L0_ffn_W2", "L0_ffn_b2", "L0_ffn_gamma", "L0_ffn_beta"]
_OUTS = [((128, 64, 256), "float32")]


def kernel(**inputs):
    import numpy as _np
    import concourse.bacc as _bacc
    from concourse import mybir as _mybir
    from concourse.bass_utils import run_bass_kernel_spmd as _run

    nc = _bacc.Bacc("TRN2", target_bir_lowering=False, num_devices=1)
    arrays, args = {}, []
    for name in _INS:
        a = _np.ascontiguousarray(inputs[name])
        arrays[f"in_{name}_dram"] = a
        args.append(nc.dram_tensor(f"in_{name}_dram", a.shape, _mybir.dt.from_np(a.dtype), kind="ExternalInput").ap())
    for i, (shape, dtype) in enumerate(_OUTS):
        dt = _mybir.dt.from_np(_np.dtype(dtype))
        args.append(nc.dram_tensor(f"out_{i}_dram", shape, dt, kind="ExternalOutput").ap())
    gnn_moe_layer_kernel(nc, *args)
    r = _run(nc, [arrays], core_ids=[0])
    got = tuple(r.results[0][f"out_{i}_dram"] for i in range(len(_OUTS)))
    return got[0]
```

```python
from contextlib import ExitStack

import concourse.bass as bass
from concourse import mybir

F32 = mybir.dt.float32
F32R = mybir.dt.float32r
BF16 = mybir.dt.bfloat16
I32 = mybir.dt.int32
U32 = mybir.dt.uint32
ALU = mybir.AluOpType
ACT = mybir.ActivationFunctionType
AX_X = mybir.AxisListType.X

P = 128
EPS = 1e-5
UNROLL = 8


class Group:

    def __init__(self, m, base):
        self.m, self.base = m, base
        self.n = base if isinstance(m, int) else m * UNROLL + base

    def plus(self, k):
        return Group(self.m, self.base + k)

    def buf(self, d):
        return self.base % d

    def before(self, d):
        return self.base // d if isinstance(self.m, int) else self.m * (UNROLL // d) + self.base // d

    def since(self, first):
        return self.base >= first


def for_groups(eng, first, last, step, known=None):
    def steps(m, bases):
        value = known(Group(m, bases[0])) if known else None
        for base in bases:
            if known:
                value = step(Group(m, base), value)
            else:
                step(Group(m, base))

    turns = (last + 1 - first) // UNROLL
    if turns > 0:
        with eng.Fori(0, turns) as m:
            steps(m, range(first, first + UNROLL))
    rest = range(first + turns * UNROLL, last + 1)
    if rest:
        steps(0, rest)


def gnn_moe_layer_kernel(nc, x, adj, Wq, bq, Wk, bk, Wv, bv, Wo, bo, Wg, W1, b1, W2, b2, gamma, beta, out):
    B, S, D = x.shape
    H = 8
    Dh = D // H
    SCALE = float(Dh) ** -0.5
    E, _, F = W1.shape
    T = B * S
    KC = D // P
    BJ = 4
    BT = BJ * P
    NBLK = T // BT
    NT = T // P
    R = 4
    GPT = P // S
    GT = 256
    GS = GT // P
    K = 2
    CARRY = 16
    ROW = D + CARRY
    CAP = T + GT
    CAPG = CAP // GT
    NG = (K * T - GT) // GT + E
    PAD0 = E * CAP
    assert GPT == KC
    assert D == 256 and F == 256 and E == 8 and S == 64 and KC == 2 and NG % 2 == 1
    assert K * T // GT + E >= NG

    xt = x.rearrange("b s d -> (b s) d").rearrange("(i j p) d -> i p j d", j=BJ, p=P)
    adjt = adj.rearrange("b s k -> (b s) k").rearrange("(i j p) k -> i p j k", j=BJ, p=P)
    outt = out.rearrange("b s d -> (b s) d").rearrange("(i j p) d -> i p j d", j=BJ, p=P)
    rows = nc.dram_tensor("expert_rows", [PAD0 + 2 * E * GT, ROW], F32, kind="Internal").ap()
    results = nc.dram_tensor("expert_results", [K * T + 2 * E * GT, D], F32, kind="Internal").ap()
    res_t = results[0:K * T, :].rearrange("(k i j p) d -> k i p j d", k=K, j=BJ, p=P)

    with ExitStack() as ctx:
        def sb(name, shape, dt=F32):
            return ctx.enter_context(nc.sbuf_tensor(name, shape, dt))

        def sem(name):
            return ctx.enter_context(nc.semaphore(name))

        bank = [ctx.enter_context(nc.psum_tensor(f"bank{n}", [P, 512], F32)) for n in range(8)]
        SBK = bank[0:4]
        W0, W1b, W2b = bank[4], bank[5], bank[7]
        RB = bank[6]
        W_ORDER = (3, 0, 1, 2)
        QKB = (W1b, W2b, W2b, W0)
        QK_ORDER = (1, 0, 2, 3)
        HB = (W0, W1b)
        CB = (SBK[2], SBK[3])

        ident = sb("ident", [P, P])
        upper = sb("upper", [P, P], BF16)
        ones = sb("ones", [P, P], BF16)
        iota_e = sb("iota_e", [P, E])
        base_e = sb("base_e", [P, E])
        ids = sb("ids", [P, NT, K], I32)
        small_rows = sb("small_rows", [22, P])
        cols = sb("cols", [P, 22])
        bvb = sb("bvb", [P, KC, P])
        boB = sb("boB", [P, D])
        projections = sb("projections", [P, 4, 2, KC, D], F32R)
        wg = sb("wg", [P, KC, E])
        we = sb("we", [P, E, 4, 256])
        b2B = sb("b2B", [P, E, D])
        gates = sb("gates", [P, NT, K])
        x2 = sb("x2", [P, NT, D])

        xin_hT2 = sb("xin_hT2", [P, 2, BJ * D])
        xin = xin_hT2[:, 0, :].rearrange("p (j d) -> p j d", j=BJ)
        hT2 = xin_hT2[:, 1, :].rearrange("p (c t) -> p c t", c=KC)
        adjs = sb("adjs", [P, BJ, S])
        xn = sb("xn", [P, BJ, D])
        xT = [sb(f"xT{part}", [P, KC, BT], F32R) for part in range(2)]
        qT = sb("qT", [P, KC, BT])
        kT = sb("kT", [P, KC, BT])
        vb = sb("vb", [P, BJ * GPT, R, 2, Dh])
        sm = sb("sm", [P, R, BT])
        mx = sb("mx", [P, R, 8])
        sums = sb("sums", [P, R, 8])
        pT = sb("pT", [P, R, BT])
        cT = [sb(f"cT{part}", [P, KC, BT], F32R) for part in range(2)]
        row = sb("row", [P, BJ, K, ROW])
        st = [sb(f"st{k}", [P, BJ, 6]) for k in range(2)]
        mv = [sb(f"mv{k}", [P, BJ, 2]) for k in range(2)]
        var = [sb(f"var{k}", [P, BJ]) for k in range(2)]
        lnv = [sb(f"lnv{k}", [P, BJ]) for k in range(2)]
        rs0 = [sb(f"rs0{k}", [P, BJ]) for k in range(2)]
        tmp = [sb(f"tmp{k}", [P, BJ]) for k in range(2)]
        rstd = [sb(f"rstd{k}", [P, BJ]) for k in range(2)]
        lgT = sb("lgT", [E, BT])
        lg = sb("lg", [P, BJ, E])
        top = sb("top", [P, BJ, 8])
        topi = sb("topi", [P, BJ, 8], U32)
        e12 = sb("e12", [P, BJ, K])
        hot = sb("hot", [P, BJ, K, E])
        both = sb("both", [P, BJ, E], BF16)
        run = sb("run", [P, E])
        runb = sb("runb", [P, E], BF16)
        blk = sb("blk", [P, E])
        place = sb("place", [P, BJ, E])
        sel = sb("sel", [P, BJ, K, E])
        dstf = sb("dstf", [P, BJ * K])
        dst = sb("dst", [P, BJ * K], I32)

        cnt = sb("cnt", [P, E])
        ngi = sb("ngi", [P, E], I32)
        ngf = sb("ngf", [P, E])
        one8 = sb("one8", [P, E])
        onesf = sb("onesf", [1, P])
        cum = sb("cum", [P, E])
        iota_g = sb("iota_g", [1, NG])
        gexp = sb("gexp", [1, NG])
        gprev = sb("gprev", [1, NG])
        tabf = sb("tabf", [1, 2, NG])
        tab = sb("tab", [1, 2, NG], I32)
        padf = sb("padf", [1, E])
        padi = sb("padi", [1, E], I32)
        zrow = hT2[:, 0, 0:D]
        pad_ids = hT2[:, 1, :].bitcast(I32).rearrange("p (e s w) -> p e s w", e=2 * E, s=GS)
        places_kept = sb("places_kept", [P, NG, GS], I32)
        yidx = [sb("yidx0", [P, GS], I32), sb("yidx1", [P, GS], I32)]
        yst = sb("yst", [P, GS, 6])
        ymv = sb("ymv", [P, GS, 2])
        yva = sb("yva", [P, GS])
        yln = sb("yln", [P, GS])
        yr0 = sb("yr0", [P, GS])
        ytm = sb("ytm", [P, GS])
        yrs = [sb("yrs0", [P, GS]), sb("yrs1", [P, GS])]

        setup_in = sem("setup_in")
        experts_in = sem("experts_in")
        pads_out = sem("pads_out")
        consts = sem("consts")
        dconst = sem("dconst")
        wo_perm = sem("wo_perm")
        su_pe = sem("su_pe")
        su_act = sem("su_act")
        w_low = sem("w_low")
        norm_in = sem("norm_in")
        bvb_done = sem("bvb_done")
        waits_passed = sem("waits_passed")
        x_in = sem("x_in")
        adj_in = sem("adj_in")
        adj_scaled = sem("adj_scaled")
        xbo_done = sem("xbo_done")
        ln1_s = sem("ln1_s")
        ln2_s = sem("ln2_s")
        var_done = sem("var_done")
        lnv_done = sem("lnv_done")
        rs0_done = sem("rs0_done")
        xn_done = sem("xn_done")
        xT_ps = sem("xT_ps")
        xT_done = sem("xT_done")
        xl_done = sem("xl_done")
        qk_ps = sem("qk_ps")
        qk_done = sem("qk_done")
        v_ps = sem("v_ps")
        v_done = sem("v_done")
        s_ps = sem("s_ps")
        masked = sem("masked")
        mx_done = sem("mx_done")
        sub_done = sem("sub_done")
        exp_done = sem("exp_done")
        sum_s = sem("sum_s")
        rsum_done = sem("rsum_done")
        prob_done = sem("prob_done")
        prob2_done = sem("prob2_done")
        pT_ps = sem("pT_ps")
        pT_done = sem("pT_done")
        c_ps = sem("c_ps")
        c_done = sem("c_done")
        cl_done = sem("cl_done")
        o_ps = sem("o_ps")
        res_done = sem("res_done")
        row_done = sem("row_done")
        row2_done = sem("row2_done")
        h_ps = sem("h_ps")
        h_done = sem("h_done")
        lgT_ps = sem("lgT_ps")
        lgT_done = sem("lgT_done")
        lg_ps = sem("lg_ps")
        rt = sem("rt")
        both_done = sem("both_done")
        place_ps = sem("place_ps")
        gd_done = sem("gd_done")
        gx_done = sem("gx_done")
        gate_step = sem("gate_step")
        dst_done = sem("dst_done")
        ids_done = sem("ids_done")
        scattered = sem("scattered")
        cnt_ps = sem("cnt_ps")
        tb = sem("tb")
        pad_at = sem("pad_at")
        tab_done = sem("tab_done")
        g_in = [sem(f"g_in{q}") for q in range(4)]
        w_cur = sem("w_cur")
        gT_ps = sem("gT_ps")
        gT_done = sem("gT_done")
        m_ps = sem("m_ps")
        m_done = sem("m_done")
        y_ps = sem("y_ps")
        yb = sem("yb")
        y_read = sem("y_read")
        yvar = sem("yvar")
        ylnv = sem("ylnv")
        yrs0 = sem("yrs0")
        yrs_done = sem("yrs_done")
        ys_done = sem("ys_done")
        kept = sem("kept")
        yidx_done = sem("yidx_done")
        yo_done = sem("yo_done")
        y_out = [sem("y_out0"), sem("y_out1")]
        r_in = [sem(f"r_in{b}") for b in range(4)]
        f_s = sem("f_s")
        f_done = sem("f_done")
        o_out = sem("o_out")

        vbf = vb[:, :, :, :, :].rearrange("p a b c d -> p (a b c d)")
        wc = [vbf[:, 512 * b:512 * b + 512].rearrange("p (k f) -> p k f", k=2) for b in range(2)]
        smf = sm[:, :, :].rearrange("p a b -> p (a b)")
        pTf = pT[:, :, :].rearrange("p a b -> p (a b)")
        ge = pTf[0:1, 0:NG * E].rearrange("p (g e) -> p g e", e=E)
        gg = pTf[0:1, 1024:1024 + NG * E].rearrange("p (g e) -> p g e", e=E)
        beB = smf.rearrange("p (e d) -> p e d", e=E)
        gaB = xin_hT2[:, :, :].rearrange("p a (e d) -> p (a e) d", d=D)
        NI = BJ
        gin = [row[:, q, :, :] for q in range(NI)]
        gT = [xn[:, 2 * b:2 * b + 2, :] for b in range(2)]
        mT = [qT[:, :, 0:GT], qT[:, :, GT:2 * GT]]
        GTB, MB, YB = SBK[0:2], SBK[2:4], (W0, W1b)
        ybuf = [kT[:, 0, :].rearrange("p (s d) -> p s d", s=GS), kT[:, 1, :].rearrange("p (s d) -> p s d", s=GS)]
        yout = [pTf[:, 0:512].rearrange("p (s d) -> p s d", s=GS), pTf[:, 512:1024].rearrange("p (s d) -> p s d", s=GS)]
        NR = 4
        rbuf = [[xin, xn], [qT[:, :, :].rearrange("p a (b d) -> p (a b) d", d=D),
                            hT2[:, :, :].rearrange("p a (b d) -> p (a b) d", d=D)]]
        for flat in (smf, pTf):
            rbuf.append([flat[:, 1024 * k:1024 * k + 1024].rearrange("p (j d) -> p j d", d=D) for k in range(K)])

        def wait_apart(eng, sem_, value):
            eng.wait_ge(sem_, value)
            eng.sem_inc(waits_passed, 1)

        def pad_experts(eng, experts):
            eng.wait_ge(pad_at, 1)
            eng.wait_ge(pads_out, 32)
            for e in experts:
                at = eng.value_load(padi[0:1, e:e + 1], min_val=e * CAP, max_val=e * CAP + T)
                eng.dma_start(rows[bass.ds(at, GT), :], rows[PAD0 + (E + e) * GT:PAD0 + (E + e + 1) * GT, :]).then_inc(pads_out, 16)

        block = ctx.enter_context(nc.Block())
        SETUP_LOADS = 4 + 3 + KC + 2
        EXPERT_LOADS = 4 + 1
        SU_BO = 6
        RT = 11
        NCONST = 11

        @block.sync
        def _(sp):
            def load(dst_, src_):
                sp.dma_start(dst_, src_).then_inc(setup_in, 16)

            sp.dma_start(xin[:, :, :], xt[0]).then_inc(x_in, 16)
            sp.dma_start(adjs[:, :, :], adjt[0]).then_inc(adj_in, 16)
            for n, w in enumerate((Wq, Wk, Wv, Wo)):
                load(pTf[:, 512 * n:512 * n + 512].rearrange("p (c e) -> p c e", c=KC),
                     w.rearrange("(c p) e -> p c e", p=P))
            load(small_rows[0:16, :], b1.rearrange("e (c p) -> (e c) p", p=P))
            load(small_rows[16:18, :], bq.rearrange("(c p) -> c p", p=P))
            load(small_rows[18:20, :], bk.rearrange("(c p) -> c p", p=P))
            bvv = bv.rearrange("(hh c r d) -> c r hh d", hh=2, c=2, r=2)
            for c in range(KC):
                load(small_rows[20 + c:21 + c, :].rearrange("o (r hh d) -> o r hh d", r=2, hh=2), bvv[c:c + 1])
            load(boB[0:1, :], bo.rearrange("(o n) -> o n", o=1))
            load(wg[:, :, :], Wg.rearrange("(c p) e -> p c e", p=P))
            def load_expert(dst_, src_):
                sp.dma_start(dst_, src_).then_inc(experts_in, 16)

            sp.wait_ge(consts, NCONST)
            padv = rows[PAD0:PAD0 + 2 * E * GT, :].rearrange("(s p) w -> p s w", p=P)
            sp.dma_start(padv[:, :, 0:D], zrow.unsqueeze(1).to_broadcast([P, 2 * E * GS, D])).then_inc(pads_out, 16)
            sp.dma_start(padv[:, :, D:ROW], hT2[:, 1, :].rearrange("p (a w) -> p a w", w=CARRY)).then_inc(pads_out, 16)

            def load_x(i):
                sp.wait_ge(xn_done, i)
                sp.wait_ge(xbo_done, i)
                sp.dma_start(xin[:, :, :], xt[bass.ds(i, 1)].rearrange("o p j d -> (o p) j d")).then_inc(x_in, 16)

            def load_mask(i):
                sp.wait_ge(masked, R * i)
                sp.dma_start(adjs[:, :, :], adjt[bass.ds(i, 1)].rearrange("o p j d -> (o p) j d")).then_inc(adj_in, 16)

            experts = [(we[:, :, 2 * l + c, :], w[:, c * P:(c + 1) * P, :].rearrange("e p f -> p e f"))
                       for l, w in enumerate((W1, W2)) for c in range(2)]
            experts.append((b2B[:, :, :], b2.partition_broadcast(P)))
            load_x(1)
            for n, (dst_, src_) in enumerate(experts):
                load_x(n + 2)
                load_mask(n + 1)
                load_expert(dst_, src_)
            with sp.Fori(EXPERT_LOADS + 1, NBLK - 1) as i:
                load_x(i + 1)
                load_mask(i)
            load_mask(NBLK - 1)
            sp.wait_ge(pT_ps, R * NBLK)
            sp.dma_start(beB, beta.partition_broadcast(P)).then_inc(norm_in, 16)
            sp.wait_ge(lgT_ps, NBLK)
            sp.dma_start(gaB, gamma.partition_broadcast(P)).then_inc(norm_in, 16)

            pad_experts(sp, range(0, E // 2))
            sp.wait_ge(tab_done, 1)
            sp.wait_ge(scattered, 16 * BJ * K * NBLK)
            sp.wait_ge(pads_out, 32 + 16 * E)

            def load_group(g):
                at = sp.value_load(tab[0:1, 0, bass.ds(g.n, 1)], min_val=0, max_val=PAD0 + (E - 1) * GT)
                sp.dma_start(gin[g.buf(NI)], rows[bass.ds(at, GT), :].rearrange("(s p) w -> p s w", p=P)).then_inc(g_in[g.buf(NI)], 16)

            def next_group(g):
                sp.wait_ge(gT_ps, g.n - NI + 1)
                sp.wait_ge(kept, g.n - NI + 1)
                load_group(g)

            for n in range(NI):
                load_group(Group(0, n))
            for_groups(sp, NI, NG - 1, next_group)
            for b in range(2):
                sp.wait_ge(y_out[b], 16 * GS * ((NG + 1 - b) // 2))

            def load_results(i, b):
                for k in range(K):
                    sp.dma_start(rbuf[b][k][:, :, :], res_t[k][bass.ds(i, 1)].rearrange("o p j d -> (o p) j d")).then_inc(r_in[b], 16)

            for b in range(NR):
                load_results(b, b)
            with sp.Fori(0, NBLK // NR - 1) as m:
                for b in range(NR):
                    sp.wait_ge(f_done, NR * m + b + 1)
                    load_results(NR * m + b + NR, b)
            sp.wait_ge(pads_out, 32 + 16 * E)

        @block.gpsimd
        def _(pool):
            def const(ins):
                ins.then_inc(consts, 1)

            const(pool.memset(ident[:, :], 0.0))
            const(pool.memset(ones[:, :], 1.0))
            const(pool.memset(zrow, 0.0))
            const(pool.memset(row[:, :, :, D:ROW], 0.0))
            const(pool.iota(ids[:, :, :], pattern=[[P, NT], [T, K]], base=0, channel_multiplier=1))
            const(pool.iota(pad_ids, pattern=[[GT, 2 * E], [P, GS], [0, CARRY]], base=K * T, channel_multiplier=1))
            const(pool.iota(iota_e[:, :], pattern=[[1, E]], base=0, channel_multiplier=0, allow_small_or_imprecise_dtypes=True))
            const(pool.iota(iota_g[:, :], pattern=[[1, NG]], base=0, channel_multiplier=0, allow_small_or_imprecise_dtypes=True))
            pool.wait_ge(consts, 8)
            const(pool.affine_select(out=ident[:, :], in_=ident[:, :], compare_op=ALU.not_equal, fill=1.0,
                                     base=0, pattern=[[-1, P]], channel_multiplier=1))
            const(pool.affine_select(out=upper[:, :], in_=ones[:, :], compare_op=ALU.is_gt, fill=0.0,
                                     base=0, pattern=[[1, P]], channel_multiplier=-1))
            const(pool.tensor_scalar(base_e[:, :], iota_e[:, :], float(CAP), None, ALU.mult))

            def scale_mask(i):
                wait_apart(pool, adj_in, 16 * i + 16)
                pool.tensor_scalar(adjs[:, :, :], adjs[:, :, :], 2.0 * SCALE, None, ALU.mult).then_inc(adj_scaled, 1)

            def x_plus_bo(i):
                wait_apart(pool, x_in, 16 * i + 16)
                pool.tensor_tensor(x2[:, bass.ds(i * BJ, BJ), :], xin[:, :, :],
                                   boB[:, :].unsqueeze(1).to_broadcast([P, BJ, D]), ALU.add).then_inc(xbo_done, 1)

            def sub_max(i):
                for r in range(R):
                    wait_apart(pool, mx_done, R * i + r + 1)
                    v = sm[:, r, :].rearrange("p (a k) -> p a k", k=S)
                    pool.tensor_tensor(v, v, mx[:, r, :].unsqueeze(2).to_broadcast([P, 8, S]), ALU.subtract).then_inc(sub_done, 1)

            def normalise(i):
                for r in (0, 1, 3):
                    wait_apart(pool, rsum_done, R * i + r + 1)
                    v = sm[:, r, :].rearrange("p (a k) -> p a k", k=S)
                    pool.tensor_tensor(v, v, sums[:, r, :].unsqueeze(2).to_broadcast([P, 8, S]), ALU.mult).then_inc(prob_done, 1)

            def carry(i):
                if not isinstance(i, int) or i > 0:
                    wait_apart(pool, scattered, 16 * BJ * K * i)
                pool.tensor_copy(row[:, :, :, D:D + 1].bitcast(I32).rearrange("p j k o -> p j (k o)"),
                                 ids[:, bass.ds(i * BJ, BJ), :]).then_inc(ids_done, 1)

            def scatter(i):
                wait_apart(pool, ids_done, i + 1)
                wait_apart(pool, dst_done, i + 1)
                wait_apart(pool, row_done, i + 1)
                wait_apart(pool, row2_done, i + 1)
                for j in range(BJ):
                    for k in range(K):
                        n = j * K + k
                        pool.indirect_dma_start(rows, bass.IndirectOffsetOnAxis(dst[:, n:n + 1], 0), row[:, j, k, :], None,
                                                bounds_check=PAD0 - 1, oob_is_err=False).then_inc(scattered, 16)

            def body(i, first=False, more=True, last=False):
                sub_max(i)
                normalise(i)
                if more:
                    x_plus_bo(i + 2)
                if not first:
                    carry(i - 1)
                    scatter(i - 1)
                if not last:
                    scale_mask(i + 1)

            pool.wait_ge(consts, NCONST)
            scale_mask(0)
            pool.wait_ge(su_act, SU_BO)
            x_plus_bo(0)
            x_plus_bo(1)
            body(0, first=True)
            with pool.Fori(1, NBLK - 2) as i:
                body(i)
            body(NBLK - 2, more=False)
            body(NBLK - 1, more=False, last=True)
            carry(NBLK - 1)
            scatter(NBLK - 1)

            def keep_places(g):
                wait_apart(pool, g_in[g.buf(NI)], 16 * g.before(NI) + 16)
                pool.tensor_copy(places_kept[:, bass.ds(g.n, 1), :].rearrange("p o s -> p (o s)"),
                                 gin[g.buf(NI)][:, :, D:D + 1].bitcast(I32).rearrange("p s o -> p (s o)")).then_inc(kept, 1)

            def finish(g):
                b = g.buf(2)
                e = pool.value_load(tab[0:1, 1, bass.ds(g.n, 1)], min_val=0, max_val=E - 1)
                wait_apart(pool, kept, g.n + 1)
                wait_apart(pool, ys_done, g.n + 1)
                pool.tensor_copy(yidx[b][:, :], places_kept[:, bass.ds(g.n, 1), :].rearrange("p o s -> p (o s)")).then_inc(yidx_done, 1)
                pool.tensor_tensor(yout[b], yout[b], beB[:, bass.ds(e, 1), :].to_broadcast([P, GS, D]), ALU.add).then_inc(yo_done, 1)
                wait_apart(pool, yo_done, g.n + 1)
                wait_apart(pool, yidx_done, g.n + 1)
                for s in range(GS):
                    pool.indirect_dma_start(results, bass.IndirectOffsetOnAxis(yidx[b][:, s:s + 1], 0), yout[b][:, s, :], None,
                                            bounds_check=K * T + 2 * E * GT - 1, oob_is_err=False).then_inc(y_out[b], 16)

            def pool_step(g):
                keep_places(g)
                finish(g.plus(-NI))

            wait_apart(pool, scattered, 16 * BJ * K * NBLK)
            pool.wait_ge(tab_done, 1)
            pool.wait_ge(norm_in, 32)
            for n in range(NI):
                keep_places(Group(0, n))
            for_groups(pool, NI, NG - 1, pool_step)
            for n in range(NG - NI, NG):
                finish(Group(0, n))
            for b in range(2):
                pool.wait_ge(y_out[b], 16 * GS * ((NG + 1 - b) // 2))

        @block.vector
        def _(dve):
            dve.memset(vb[:, :, :, :, :].rearrange("p a b c d -> p (a b c d)"), 0.0).then_inc(dconst, 1)
            dve.memset(onesf[:, :], 1.0).then_inc(dconst, 1)
            dve.memset(one8[:, :], 1.0).then_inc(dconst, 1)
            dve.memset(run[:, :], 0.0).then_inc(dconst, 1)
            dve.memset(runb[:, :], 0.0).then_inc(dconst, 1)
            LN = 6

            LN_S = (ln1_s, ln2_s)

            def tile_stats(k, src, tiles, last):
                for j in tiles:
                    ins = dve.bn_stats(st[k][:, j, :], src(j))
                if last:
                    ins.then_inc(LN_S[k], 1)

            def variance(n, k):
                wait_apart(dve, LN_S[k], LN * n + 1)
                for j in range(BJ):
                    ins = dve.bn_aggr(mv[k][:, j, :], st[k][:, j, :])
                ins.then_inc(LN_S[k], 1)
                dve.wait_ge(LN_S[k], LN * n + 2)
                dve.tensor_scalar(var[k][:, :], mv[k][:, :, 1], EPS, None, ALU.add).then_inc(var_done, 1)

            def deviation(n, count, k, step):
                if step == 0:
                    dve.wait_ge(rs0_done, count)
                    dve.tensor_tensor(tmp[k][:, :], var[k][:, :], rs0[k][:, :], ALU.mult).then_inc(LN_S[k], 1)
                elif step == 1:
                    dve.wait_ge(LN_S[k], LN * n + 3)
                    dve.tensor_tensor(tmp[k][:, :], tmp[k][:, :], rs0[k][:, :], ALU.mult).then_inc(LN_S[k], 1)
                elif step == 2:
                    dve.wait_ge(LN_S[k], LN * n + 4)
                    dve.tensor_scalar(tmp[k][:, :], tmp[k][:, :], -0.5, 1.5, ALU.mult, ALU.add).then_inc(LN_S[k], 1)
                else:
                    dve.wait_ge(LN_S[k], LN * n + 5)
                    dve.tensor_tensor(rstd[k][:, :], tmp[k][:, :], rs0[k][:, :], ALU.mult).then_inc(LN_S[k], 1)

            def scale_rows(n, k, src, out_, used, done):
                if not isinstance(n, int) or n > 0:
                    dve.wait_ge(used[0], used[1] * n)
                wait_apart(dve, LN_S[k], LN * n + 6)
                for j in range(BJ):
                    ins = dve.tensor_scalar(out_(j), src(j), mv[k][:, j, 0:1], rstd[k][:, j:j + 1], ALU.subtract, ALU.mult)
                ins.then_inc(done, 1)

            def x_row(j):
                return xin[:, j, :]

            def ln1_stats(i):
                wait_apart(dve, x_in, 16 * i + 16)
                tile_stats(0, x_row, range(BJ), last=True)

            def ln1_start(i):
                ln1_stats(i)
                variance(i, 0)

            def ln1_step(i, step):
                deviation(i, LN1_AT(i), 0, step)

            def ln1_steps(i):
                for step in range(4):
                    ln1_step(i, step)

            def ln1_end(i):
                scale_rows(i, 0, x_row, lambda j: xn[:, j, :], (xT_ps, KC), xn_done)

            def LN1_AT(n):
                return n + 1 if isinstance(n, int) and n < 3 else 2 * n - 2

            def LN2_AT(n):
                return NBLK + n + 1 if isinstance(n, int) and n >= NBLK - 3 else 2 * n + 5

            def ln2(i):
                variance(i, 1)
                for step in range(4):
                    deviation(i, LN2_AT(i), 1, step)
                scale_rows(i, 1, lambda j: x2_row(i, j), lambda j: row[:, j, 0, 0:D], (scattered, 16 * BJ * K), row_done)

            def x_lows(i):
                for c in range(KC):
                    dve.wait_ge(xT_done, KC * i + c + 1)
                    dve.tensor_tensor(xT[1][:, c, :], SBK[c][:, :], xT[0][:, c, :].bitcast(F32), ALU.subtract).then_inc(xl_done, 1)

            def c_low(i, c):
                dve.wait_ge(c_done, KC * i + c + 1)
                dve.tensor_tensor(cT[1][:, c, :], CB[c][:, :], cT[0][:, c, :].bitcast(F32), ALU.subtract).then_inc(cl_done, 1)

            def mask_and_max(i):
                dve.wait_ge(adj_scaled, i + 1)
                dve.wait_ge(s_ps, i + 1)

                def mask(r):
                    a = adjs[:, :, :].unsqueeze(2).to_broadcast([P, BJ, 2, S])
                    dve.tensor_tensor(sm[:, r, :].rearrange("p (j h k) -> p j h k", j=BJ, h=2),
                                      SBK[r][:, :].rearrange("p (j h k) -> p j h k", j=BJ, h=2), a, ALU.mult).then_inc(masked, 1)

                mask(0)
                for r in range(R):
                    if r + 1 < R:
                        mask(r + 1)
                    dve.wait_ge(masked, R * i + r + 1)
                    dve.tensor_reduce(mx[:, r, :], sm[:, r, :].rearrange("p (a k) -> p a k", k=S), AX_X, ALU.max).then_inc(mx_done, 1)

            def prob_sums(i):
                for r in range(R):
                    dve.wait_ge(exp_done, R * i + r + 1)
                    dve.tensor_reduce(sums[:, r, :], sm[:, r, :].rearrange("p (a k) -> p a k", k=S), AX_X, ALU.add).then_inc(sum_s, 1)
                    dve.wait_ge(sum_s, R * i + r + 1)
                    dve.reciprocal(sums[:, r, :], sums[:, r, :]).then_inc(rsum_done, 1)
                dve.wait_ge(rsum_done, R * i + 3)
                v = sm[:, 2, :].rearrange("p (a k) -> p a k", k=S)
                dve.tensor_tensor(v, v, sums[:, 2, :].unsqueeze(2).to_broadcast([P, 8, S]), ALU.mult).then_inc(prob2_done, 1)

            def route_a(i, ahead=None):
                n = 0
                dve.wait_ge(lg_ps, i + 1)
                dve.tensor_copy(lg[:, :, :].rearrange("p j e -> p (j e)"), RB[:, 0:BJ * E]).then_inc(rt, 1)
                if ahead is not None:
                    ln1_step(ahead, 0)
                wait_apart(dve, rt, RT * i + 1)
                for j in range(BJ):
                    ins = dve.max(top[:, j, :], lg[:, j, :])
                ins.then_inc(rt, 1)
                if ahead is not None:
                    ln1_step(ahead, 1)
                wait_apart(dve, rt, RT * i + 2)
                for j in range(BJ):
                    ins = dve.max_index(topi[:, j, :], top[:, j, :], lg[:, j, :])
                ins.then_inc(rt, 1)
                dve.tensor_tensor(gates[:, bass.ds(i * BJ, BJ), 1:2].rearrange("p j o -> p (j o)"), top[:, :, 1], top[:, :, 0],
                                  ALU.subtract).then_inc(gd_done, 1)
                if ahead is not None:
                    ln1_step(ahead, 2)
                dve.wait_ge(rt, RT * i + 3)
                dve.tensor_copy(e12[:, :, :], topi[:, :, 0:K]).then_inc(rt, 1)
                if ahead is not None:
                    ln1_step(ahead, 3)
                dve.wait_ge(rt, RT * i + 4)
                dve.tensor_tensor(hot[:, :, :, :].rearrange("p j k e -> p (j k) e"),
                                  iota_e[:, :].unsqueeze(1).to_broadcast([P, BJ * K, E]),
                                  e12[:, :, :].rearrange("p j k -> p (j k)").unsqueeze(2).to_broadcast([P, BJ * K, E]),
                                  ALU.is_equal).then_inc(rt, 1)
                dve.wait_ge(rt, RT * i + 5)
                dve.tensor_tensor(both[:, :, :], hot[:, :, 0, :], hot[:, :, 1, :], ALU.add).then_inc(both_done, 1)

            def route_b(i):
                dve.wait_ge(place_ps, i + 1)
                dve.tensor_tensor(place[:, :, :], RB[:, 64:64 + BJ * E].rearrange("p (j e) -> p j e", j=BJ),
                                  base_e[:, :].unsqueeze(1).to_broadcast([P, BJ, E]), ALU.add).then_inc(rt, 1)
                dve.tensor_reduce(blk[:, :], both[:, :, :].rearrange("p j e -> p e j"), AX_X, ALU.add).then_inc(rt, 1)
                dve.wait_ge(rt, RT * i + 6)
                dve.tensor_tensor(sel[:, :, :, :], hot[:, :, :, :], place[:, :, :].unsqueeze(2).to_broadcast([P, BJ, K, E]),
                                  ALU.mult).then_inc(rt, 1)
                dve.wait_ge(rt, RT * i + 7)
                dve.tensor_tensor(run[:, :], run[:, :], blk[:, :], ALU.add).then_inc(rt, 1)
                dve.wait_ge(rt, RT * i + 8)
                dve.tensor_reduce(dstf[:, :], sel[:, :, :, :].rearrange("p j k e -> p (j k) e"), AX_X, ALU.add).then_inc(rt, 1)
                dve.wait_ge(rt, RT * i + 9)
                dve.tensor_copy(runb[:, :], run[:, :]).then_inc(rt, 1)
                dve.wait_ge(rt, RT * i + 10)
                if not isinstance(i, int) or i > 0:
                    dve.wait_ge(scattered, 16 * BJ * K * i)
                dve.tensor_copy(dst[:, :], dstf[:, :]).then_inc(dst_done, 1)

            def gate_values():
                first_, second = gates[:, :, 0], gates[:, :, 1]
                dve.wait_ge(gx_done, 1)
                dve.tensor_scalar(first_, second, 1.0, None, ALU.add).then_inc(gate_step, 1)
                dve.wait_ge(gate_step, 1)
                dve.reciprocal(first_, first_).then_inc(gate_step, 1)
                dve.wait_ge(gate_step, 2)
                dve.tensor_tensor(second, second, first_, ALU.mult).then_inc(gate_step, 1)
                dve.wait_ge(gate_step, 3)

            def x2_row(i, j):
                return x2[:, bass.ds(i * BJ + j, 1), :].rearrange("p o d -> p (o d)")

            def residual(i, jj):
                dve.wait_ge(o_ps, 2 * i + jj + 1)
                v = x2[:, bass.ds(i * BJ + 2 * jj, 2), :].rearrange("p j d -> p (j d)")
                dve.tensor_tensor(v, (W0, W1b)[jj][:, :], v, ALU.add).then_inc(res_done, 1)

            def residual_stats(i, jj):
                wait_apart(dve, res_done, 2 * i + jj + 1)
                tile_stats(1, lambda j: x2_row(i, j), (2 * jj, 2 * jj + 1), last=(jj == 1))

            def rest_of_residual(i):
                residual(i, 1)
                residual_stats(i, 1)
                ln2(i)

            def body(i, first=False, more=True):
                if more:
                    ln1_stats(i + 2)
                if not first:
                    residual_stats(i - 1, 0)
                if more:
                    variance(i + 2, 0)
                if not first:
                    rest_of_residual(i - 1)
                mask_and_max(i)
                prob_sums(i)
                if not first:
                    route_a(i - 1, ahead=(i + 2 if more else None))
                elif more:
                    ln1_steps(i + 2)
                if more:
                    ln1_end(i + 2)
                if not first:
                    route_b(i - 1)
                c_low(i, 0)
                c_low(i, 1)
                if more:
                    x_lows(i + 2)
                dve.wait_ge(xbo_done, i + 1)
                residual(i, 0)

            ln1_start(0)
            ln1_steps(0)
            ln1_end(0)

            dve.wait_ge(setup_in, 16 * SETUP_LOADS)
            wo_nat = pTf[:, 1536:2048].rearrange("p (f hh c r d) -> p f c r hh d", f=KC, hh=2, c=KC, r=2)
            for f in range(KC):
                for c in range(KC):
                    o = smf[:, (f * KC + c) * P:(f * KC + c + 1) * P].rearrange("p (r hh d) -> p r hh d", r=2, hh=2)
                    ins = dve.tensor_copy(o, wo_nat[:, f, c])
            ins.then_inc(wo_perm, 1)
            dve.wait_ge(su_act, 1)
            for c in range(KC):
                ins = dve.tensor_copy(bvb[:, c, :], cols[:, 20 + c:21 + c].to_broadcast([P, P]))
            ins.then_inc(bvb_done, 1)
            for k, n in enumerate(W_ORDER):
                dve.wait_ge(su_act, k + 2)
                dve.tensor_tensor(projections[:, n, 1, :, :].rearrange("p c f -> p (c f)"), SBK[n][:, :],
                                  projections[:, n, 0, :, :].bitcast(F32).rearrange("p c f -> p (c f)"), ALU.subtract).then_inc(w_low, 1)

            x_lows(0)
            ln1_start(1)
            ln1_steps(1)
            ln1_end(1)
            x_lows(1)
            body(0, first=True)
            with dve.Fori(1, NBLK - 2) as i:
                body(i)
            body(NBLK - 2, more=False)
            body(NBLK - 1, more=False)
            residual_stats(NBLK - 1, 0)
            rest_of_residual(NBLK - 1)
            route_a(NBLK - 1)
            route_b(NBLK - 1)

            tn = [0]

            def t(ins):
                tn[0] += 1
                ins.then_inc(tb, 1)
                dve.wait_ge(tb, tn[0])

            dve.wait_ge(cnt_ps, 1)
            t(dve.tensor_copy(cnt[:, :], RB[:, 0:E]))
            t(dve.tensor_tensor(padf[:, :], cnt[0:1, :], base_e[0:1, :], ALU.add))
            dve.tensor_copy(padi[:, :], padf[:, :]).then_inc(pad_at, 1)
            t(dve.tensor_scalar(ngf[:, :], cnt[:, :], float(GT - 1), None, ALU.add))
            t(dve.tensor_copy(ngi[:, :], ngf[:, :]))
            t(dve.tensor_scalar(ngi[:, :], ngi[:, :], GT.bit_length() - 1, None, ALU.logical_shift_right))
            t(dve.tensor_copy(ngf[:, :], ngi[:, :]))
            t(dve.tensor_tensor_scan(cum[:, :], one8[:, :], ngf[:, :], 0.0, ALU.mult, ALU.add))
            t(dve.tensor_tensor(ge, iota_g[:, :].unsqueeze(2).to_broadcast([1, NG, E]),
                                cum[0:1, :].unsqueeze(1).to_broadcast([1, NG, E]), ALU.is_ge))
            t(dve.tensor_tensor(gg, ge, ngf[0:1, :].unsqueeze(1).to_broadcast([1, NG, E]), ALU.mult))
            t(dve.tensor_reduce(gexp[:, :], ge, AX_X, ALU.add))
            t(dve.tensor_reduce(gprev[:, :], gg, AX_X, ALU.add))
            t(dve.tensor_scalar(tabf[:, 0, :], gexp[:, :], float(CAPG), None, ALU.mult))
            t(dve.tensor_tensor(tabf[:, 0, :], tabf[:, 0, :], gprev[:, :], ALU.subtract))
            t(dve.tensor_tensor(tabf[:, 0, :], tabf[:, 0, :], iota_g[:, :], ALU.add))
            t(dve.tensor_scalar(tabf[:, 0, :], tabf[:, 0, :], float(GT), None, ALU.mult))
            t(dve.tensor_scalar(tabf[:, 1, :], gexp[:, :], float(E - 1), None, ALU.min))
            dve.tensor_copy(tab[:, :, :], tabf[:, :, :]).then_inc(tab_done, 1)
            gate_values()

            def expert_of(g):
                return dve.value_load(tab[0:1, 1, bass.ds(g.n, 1)], min_val=0, max_val=E - 1)

            def group(g, e):
                n, b = g.n, g.buf(2)
                if g.since(2):
                    dve.wait_ge(ys_done, n - 1)
                dve.wait_ge(y_ps, n + 1)
                dve.tensor_tensor(ybuf[b], YB[b][:, :].rearrange("p (s d) -> p s d", s=GS),
                                  b2B[:, bass.ds(e, 1), :].to_broadcast([P, GS, D]), ALU.add).then_inc(y_read, 1)
                wait_apart(dve, y_read, n + 1)
                for q in range(GS):
                    ins = dve.bn_stats(yst[:, q, :], ybuf[b][:, q, :])
                ins.then_inc(yb, 1)
                wait_apart(dve, yb, YS * n + 1)
                for q in range(GS):
                    ins = dve.bn_aggr(ymv[:, q, :], yst[:, q, :])
                ins.then_inc(yb, 1)
                dve.wait_ge(yb, YS * n + 2)
                dve.tensor_scalar(yva[:, :], ymv[:, :, 1], EPS, None, ALU.add).then_inc(yvar, 1)
                for q in range(GS):
                    dve.scalar_tensor_tensor(ybuf[b][:, q, :], ybuf[b][:, q, :], ymv[:, q, 0:1],
                                             gaB[:, bass.ds(e, 1), :].rearrange("p o d -> p (o d)"), ALU.subtract, ALU.mult)
                next_e = expert_of(g.plus(1)) if not isinstance(g.m, int) or g.base < NG - 1 else None
                dve.wait_ge(yrs0, n + 1)
                dve.tensor_tensor(ytm[:, :], yva[:, :], yr0[:, :], ALU.mult).then_inc(yb, 1)
                dve.wait_ge(yb, YS * n + 3)
                dve.tensor_tensor(ytm[:, :], ytm[:, :], yr0[:, :], ALU.mult).then_inc(yb, 1)
                dve.wait_ge(yb, YS * n + 4)
                dve.tensor_scalar(ytm[:, :], ytm[:, :], -0.5, 1.5, ALU.mult, ALU.add).then_inc(yb, 1)
                dve.wait_ge(yb, YS * n + 5)
                dve.tensor_tensor(yrs[b][:, :], ytm[:, :], yr0[:, :], ALU.mult).then_inc(yrs_done, 1)
                return next_e

            YS = 5
            dve.wait_ge(tab_done, 1)
            dve.wait_ge(experts_in, 16 * EXPERT_LOADS)
            dve.wait_ge(norm_in, 32)
            e = expert_of(Group(0, 0))
            for n in range(2):
                e = group(Group(0, n), e)
            for_groups(dve, 2, NG - 1, group, known=expert_of)

            def combine(i, nb, b):
                dve.wait_ge(r_in[b], 16 * K * (nb + 1))
                for k in range(K):
                    for j in range(BJ):
                        v = x2[:, bass.ds(i * BJ + j, 1), :].rearrange("p o d -> p (o d)")
                        g = gates[:, bass.ds(i * BJ + j, 1), k:k + 1].rearrange("p o k -> p (o k)")
                        ins = dve.scalar_tensor_tensor(v, rbuf[b][k][:, j, :], g, v, ALU.mult, ALU.add)
                    if k == 0:
                        ins.then_inc(f_s, 1)
                        dve.wait_ge(f_s, i + 1)
                ins.then_inc(f_done, 1)

            with dve.Fori(0, NBLK // NR) as m:
                for b in range(NR):
                    combine(NR * m + b, m, b)

        @block.scalar
        def _(act):
            nc.scalar.preload_act_table_set("natural_log_exp_and_others")

            def copy(o, i_, sem_):
                act.activation(o, i_, ACT.Copy).then_inc(sem_, 1)

            def rsqrt_start(n, k):
                act.wait_ge(var_done, n + 1)
                act.activation(lnv[k][:, :], var[k][:, :], ACT.Ln).then_inc(lnv_done, 1)
                act.wait_ge(lnv_done, n + 1)
                act.activation(rs0[k][:, :], lnv[k][:, :], ACT.Exp, scale=-0.5).then_inc(rs0_done, 1)

            def x_copies(i):
                for c in range(KC):
                    act.wait_ge(xT_ps, KC * i + c + 1)
                    copy(xT[0][:, c, :], SBK[c][:, :], xT_done)

            def qk_copy(i, n):
                m = QK_ORDER[n]
                act.wait_ge(qk_ps, 4 * i + n + 1)
                act.activation((qT, kT)[m // 2][:, m % 2, :], QKB[m][:, :], ACT.Identity,
                               bias=cols[:, 16 + m:17 + m]).then_inc(qk_done, 1)

            def exps(i, r):
                act.wait_ge(sub_done, R * i + r + 1)
                act.activation(sm[:, r, :], sm[:, r, :], ACT.Exp).then_inc(exp_done, 1)

            def v_copies(i, jj):
                act.wait_ge(v_ps, 2 * i + jj + 1)
                for g in range(GPT):
                    for hh in range(2):
                        src = (W1b, W2b)[jj][S * g:S * g + S, :].rearrange("p (j h r d) -> p j h r d", j=2, h=2, r=R)[:, :, hh]
                        o = vb[S * hh:S * hh + S, :, :, hh, :].rearrange("p (j g) r d -> p j g r d", g=GPT)[:, 2 * jj:2 * jj + 2, g]
                        ins = act.activation(o, src, ACT.Copy)
                ins.then_inc(v_done, 1)

            def lgT_copy(i):
                act.wait_ge(lgT_ps, i + 1)
                copy(lgT[:, :], RB[0:E, :], lgT_done)

            def h_copies(i):
                if isinstance(i, int) and i == 0:
                    act.wait_ge(pads_out, 32)
                for c in range(KC):
                    act.wait_ge(h_ps, KC * i + c + 1)
                    copy(hT2[:, c, :], HB[c][:, :], h_done)

            def second_rows(i):
                act.wait_ge(row_done, i + 1)
                act.activation(row[:, :, 1, 0:D], row[:, :, 0, 0:D], ACT.Copy).then_inc(row2_done, 1)

            def c_copy(i, c):
                act.wait_ge(c_ps, KC * i + c + 1)
                copy(cT[0][:, c, :], CB[c][:, :], c_done)

            def body(i, first=False, more=True, last=False):
                if more:
                    rsqrt_start(2 if first else 2 * i + 1, 0)
                if not first:
                    rsqrt_start(2 * i + 2 if more else NBLK + i - 1, 1)
                if not last:
                    act.wait_ge(s_ps, i + 1)
                    qk_copy(i + 1, 0)
                    qk_copy(i + 1, 1)
                if not first:
                    h_copies(i - 1)
                if not last:
                    qk_copy(i + 1, 2)
                exps(i, 0)
                if not last:
                    qk_copy(i + 1, 3)
                exps(i, 1)
                exps(i, 2)
                if not first:
                    lgT_copy(i - 1)
                exps(i, 3)
                if not first:
                    second_rows(i - 1)
                for r in range(R):
                    act.wait_ge(pT_ps, R * i + r + 1)
                    copy(pT[:, r, :], SBK[r][:, :], pT_done)
                c_copy(i, 0)
                c_copy(i, 1)
                if more:
                    act.wait_ge(v_ps, 2 * i + 4)
                    x_copies(i + 2)
                if not last:
                    v_copies(i + 1, 0)
                    v_copies(i + 1, 1)

            rsqrt_start(0, 0)
            act.wait_ge(su_pe, 1)
            copy(cols[:, :], W0[:, 0:22], su_act)
            for k, n in enumerate(W_ORDER):
                act.wait_ge(su_pe, k + 2)
                copy(projections[:, n, 0, :, :].rearrange("p c f -> p (c f)"), SBK[n][:, :], su_act)
            act.wait_ge(su_pe, 6)
            copy(boB[:, :], W1b[:, 0:D], su_act)
            act.wait_ge(dconst, 5)
            x_copies(0)
            for m in range(4):
                qk_copy(0, m)
            rsqrt_start(1, 0)
            act.wait_ge(v_ps, 2)
            x_copies(1)
            for jj in range(2):
                v_copies(0, jj)
            body(0, first=True)
            with act.Fori(1, NBLK - 2) as i:
                body(i)
            body(NBLK - 2, more=False)
            body(NBLK - 1, more=False, last=True)
            rsqrt_start(2 * NBLK - 1, 1)
            h_copies(NBLK - 1)
            lgT_copy(NBLK - 1)
            second_rows(NBLK - 1)
            act.wait_ge(gd_done, NBLK)
            act.activation(gates[:, :, 1], gates[:, :, 1], ACT.Exp).then_inc(gx_done, 1)

            def expert_of(g):
                return act.value_load(tab[0:1, 1, bass.ds(g.n, 1)], min_val=0, max_val=E - 1)

            def weights(e, g):
                act.activation(wc[g.buf(2)], we[:, bass.ds(e, 1), 0:2, :].rearrange("p o k f -> p (o k) f"),
                               ACT.Copy).then_inc(w_cur, 1)

            def g_copy(g):
                act.wait_ge(gT_ps, g.n + 1)
                act.activation(gT[g.buf(2)], GTB[g.buf(2)][:, :].rearrange("p (k t) -> p k t", k=KC), ACT.Copy).then_inc(gT_done, 1)

            def hidden(g, e):
                act.wait_ge(m_ps, g.n + 1)
                for c in range(2):
                    act.activation(mT[g.buf(2)][:, c, :], MB[g.buf(2)][:, c * GT:(c + 1) * GT], ACT.Relu,
                                   bias=cols[:, bass.ds(e * 2 + c, 1)]).then_inc(m_done, 1)

            def y_rsqrt(g):
                act.wait_ge(yvar, g.n + 1)
                act.activation(yln[:, :], yva[:, :], ACT.Ln).then_inc(ylnv, 1)
                act.wait_ge(ylnv, g.n + 1)
                act.activation(yr0[:, :], yln[:, :], ACT.Exp, scale=-0.5).then_inc(yrs0, 1)

            def y_scale(g):
                b = g.buf(2)
                act.wait_ge(yrs_done, g.n + 1)
                if g.since(2):
                    act.wait_ge(y_out[b], 16 * GS * g.before(2))
                for q in range(GS):
                    ins = act.activation(yout[b][:, q, :], ybuf[b][:, q, :], ACT.Copy, scale=yrs[b][:, q:q + 1])
                ins.then_inc(ys_done, 1)

            def act_step(g, e):
                more, next_ = g.base < NG - 2, g.base < NG - 1
                if not isinstance(g.m, int):
                    more = next_ = True
                if more:
                    act.wait_ge(m_ps, g.n + 1)
                    g_copy(g.plus(2))
                if g.since(2):
                    y_scale(g.plus(-2))
                if more:
                    e2 = expert_of(g.plus(2))
                    weights(e2, g.plus(2))
                else:
                    e2 = None
                if next_:
                    if g.since(1):
                        act.wait_ge(y_ps, g.n)
                    hidden(g.plus(1), e)
                if g.since(1):
                    y_rsqrt(g.plus(-1))
                return e2

            pad_experts(act, range(E // 2, E))
            act.wait_ge(tab_done, 1)
            act.wait_ge(experts_in, 16 * EXPERT_LOADS)
            group0, group1 = Group(0, 0), Group(0, 1)
            e0 = expert_of(group0)
            e1 = expert_of(group1)
            weights(e0, group0)
            weights(e1, group1)
            g_copy(group0)
            g_copy(group1)
            hidden(group0, e0)
            e = e1
            for n in range(4):
                e = act_step(Group(0, n), e)
            for_groups(act, 4, NG - 3, act_step, known=lambda g: expert_of(g.plus(1)))
            e = act_step(Group(0, NG - 2), expert_of(Group(0, NG - 1)))
            act_step(Group(0, NG - 1), e)
            y_scale(Group(0, NG - 2))
            y_rsqrt(Group(0, NG - 1))
            y_scale(Group(0, NG - 1))

            with act.Fori(0, NBLK) as i:
                act.wait_ge(f_done, i + 1)
                act.dma_start(outt[bass.ds(i, 1)].rearrange("o p j d -> (o p) j d"),
                              x2[:, bass.ds(i * BJ, BJ), :]).then_inc(o_out, 16)
            act.wait_ge(o_out, 16 * NBLK)

        @block.tensor
        def _(pe):
            pe.wait_ge(consts, NCONST)
            pe.wait_ge(setup_in, 16 * SETUP_LOADS)
            pe.transpose(W0[:, 0:22], small_rows[:, :], ident[0:22, 0:22]).then_inc(su_pe, 1)
            for n in W_ORDER:
                if n == 3:
                    pe.wait_ge(wo_perm, 1)
                nat = (pTf[:, 512 * n:512 * n + 512] if n < 3 else smf[:, 0:512]).rearrange("p (f e) -> p f e", f=KC)
                for c in range(KC):
                    for f in range(KC):
                        mm = pe.transpose(SBK[n][:, c * D + f * P:c * D + (f + 1) * P], nat[:, f, c * P:(c + 1) * P], ident[:, :])
                mm.then_inc(su_pe, 1)
            pe.wait_ge(bvb_done, 1)
            pe.wait_ge(su_act, 2)
            pe.wait_ge(dconst, 5)
            pe.wait_ge(w_low, 1)
            for c in range(KC):
                for part in range(2):
                    pe.matmul(W1b[:, 0:D], bvb[:, c, :], projections[:, 3, part, c, :].bitcast(F32), start=(c == 0 and part == 0), stop=False)
            pe.matmul(W1b[:, 0:D], onesf[:, :], boB[0:1, :], start=False, stop=True).then_inc(su_pe, 1)

            def in_parts(out_, stationary, moving, cs=range(KC)):
                for c in cs:
                    for a, b in ((0, 0), (0, 1), (1, 0)):
                        mm = pe.matmul(out_, stationary(a, c), moving(b, c), start=(c == 0 and a + b == 0), stop=(c == KC - 1 and a == 1))
                return mm

            def x_transposes(i):
                pe.wait_ge(xn_done, i + 1)
                for c in range(KC):
                    if not isinstance(i, int) or i > 1:
                        pe.wait_ge(pT_done, R * (i - 2) + c + 1)
                    for j in range(BJ):
                        mm = pe.transpose(SBK[c][:, j * P:(j + 1) * P], xn[:, j, c * P:(c + 1) * P], ident[:, :])
                    mm.then_inc(xT_ps, 1)

            def qk(i, n, t, cs=range(KC)):
                if t == 0 and 0 in cs:
                    if n == 0:
                        pe.wait_ge(xl_done, KC * i + KC)
                        if not isinstance(i, int) or i > 0:
                            pe.wait_ge(v_done, 2 * i)
                    elif n == 1 and (not isinstance(i, int) or i > 1):
                        pe.wait_ge(res_done, 2 * (i - 1))
                    elif n == 2:
                        pe.wait_ge(qk_done, 4 * i + 1)
                    elif n == 3 and (not isinstance(i, int) or i > 1):
                        pe.wait_ge(h_done, KC * (i - 2) + 1)
                m = QK_ORDER[n]
                mm = in_parts(QKB[m][:, t * 256:t * 256 + 256], lambda part, c: projections[:, m // 2, part, c, (m % 2) * P:(m % 2 + 1) * P],
                              lambda part, c: xT[part][:, c, t * 256:t * 256 + 256], cs)
                if t == 1 and KC - 1 in cs:
                    mm.then_inc(qk_ps, 1)

            def v(i, jj, tiles=range(2)):
                if jj == 0 and 0 in tiles:
                    pe.wait_ge(qk_done, 4 * i + 4)
                for j in tiles:
                    t0 = (2 * jj + j) * P
                    mm = in_parts((W1b, W2b)[jj][:, j * D:(j + 1) * D], lambda part, c: xT[part][:, c, t0:t0 + P],
                                  lambda part, c: projections[:, 2, part, c, :])
                if 1 in tiles:
                    mm.then_inc(v_ps, 1)

            def scores(i, first, last):
                pe.wait_ge(qk_done, 4 * i + 4)
                if not isinstance(i, int) or i > 0:
                    pe.wait_ge(pT_done, R * i)
                for j in range(BJ):
                    for g in range(GPT):
                        if not first and j < 2:
                            output(i - 1, 1, j, (g,))
                        if j == 0 and g == 0 and not last:
                            pe.wait_ge(xl_done, KC * (i + 2))
                        if j >= 2 and not last:
                            qk(i + 1, 0, j - 2, (g,))
                        t0 = j * P + g * S
                        for hh in range(2):
                            for r in range(R):
                                mm = pe.matmul(SBK[r][S * g:S * g + S, (2 * j + hh) * S:(2 * j + hh + 1) * S],
                                               qT[Dh * r:Dh * r + Dh, hh, t0:t0 + S], kT[Dh * r:Dh * r + Dh, hh, t0:t0 + S],
                                               start=True, stop=True)
                mm.then_inc(s_ps, 1)

            def row_transposes(i):
                pe.wait_ge(row_done, i + 1)
                for c in range(KC):
                    if c == 1 and not (isinstance(i, int) and i >= NBLK - 2):
                        pe.wait_ge(qk_done, 4 * (i + 2) + 2)
                    for j in range(BJ):
                        mm = pe.transpose(HB[c][:, j * P:(j + 1) * P], row[:, j, 0, c * P:(c + 1) * P], ident[:, :])
                    mm.then_inc(h_ps, 1)

            def logits(i):
                pe.wait_ge(h_done, KC * i + KC)
                for c in range(KC):
                    mm = pe.matmul(RB[0:E, :], wg[:, c, :], hT2[:, c, :], start=(c == 0), stop=(c == KC - 1))
                mm.then_inc(lgT_ps, 1)

            def logits_back(i):
                wait_apart(pe, lgT_done, i + 1)
                for j in range(BJ):
                    mm = pe.transpose(RB[:, j * E:(j + 1) * E], lgT[:, j * P:(j + 1) * P], ident[0:E, 0:E])
                mm.then_inc(lg_ps, 1)

            def places(i):
                pe.wait_ge(both_done, i + 1)
                o = RB[:, 64:64 + BJ * E]
                pe.matmul(o, upper[:, :], both[:, :, :].rearrange("p j e -> p (j e)"), start=True, stop=False, skip_group_check=True)
                for j in range(BJ - 1):
                    w = BJ - 1 - j
                    pe.matmul(RB[:, 64 + (j + 1) * E:64 + BJ * E].rearrange("p (j e) -> p j e", j=w), ones[:, :],
                              both[:, j, :].unsqueeze(1).to_broadcast([P, w, E]), start=False, stop=False, skip_group_check=True)
                pe.matmul(o.rearrange("p (j e) -> p j e", j=BJ), ones[:, :], runb[:, :].unsqueeze(1).to_broadcast([P, BJ, E]),
                          start=False, stop=True, skip_group_check=True).then_inc(place_ps, 1)

            def prob_transposes(i, last):
                for r in range(R):
                    if r in (1, 3) and not last:
                        v(i + 1, 1, (r // 2,))
                    if r == 2:
                        pe.wait_ge(prob2_done, i + 1)
                    else:
                        pe.wait_ge(prob_done, (R - 1) * i + min(r, 2) + 1)
                    for j in range(BJ):
                        mm = pe.transpose(SBK[r][:, j * P:(j + 1) * P], sm[:, r, j * P:(j + 1) * P], ident[:, :])
                    mm.then_inc(pT_ps, 1)

            def context(i, c):
                pe.wait_ge(pT_done, R * i + 3 + c)
                if c == 0:
                    pe.wait_ge(v_done, 2 * i + 2)
                for j in range(BJ):
                    for g in range(GPT):
                        t0 = j * P + g * S
                        for r2 in range(2):
                            mm = pe.matmul(CB[c][S * r2:S * r2 + S, t0:t0 + S],
                                           vb[:, 2 * j + g, 2 * c + r2, :, :].rearrange("p h d -> p (h d)"),
                                           pT[:, 2 * c + r2, t0:t0 + S], start=True, stop=True)
                mm.then_inc(c_ps, 1)

            def output(i, jj, j, cs=range(KC)):
                if jj == 0:
                    if j == 0:
                        pe.wait_ge(cl_done, KC * i + max(cs) + 1)
                elif j == 0 and 0 in cs and not (isinstance(i, int) and i == NBLK - 1):
                    pe.wait_ge(v_done, 2 * i + 3)
                t0 = (2 * jj + j) * P
                mm = in_parts((W0, W1b)[jj][:, j * D:(j + 1) * D], lambda part, c: cT[part][:, c, t0:t0 + P],
                              lambda part, c: projections[:, 3, part, c, :], cs)
                if j == 1 and KC - 1 in cs:
                    mm.then_inc(o_ps, 1)

            def body(i, first=False, more=True, last=False):
                scores(i, first, last)
                if not last:
                    for t in range(2):
                        qk(i + 1, 1, t)
                if not first:
                    row_transposes(i - 1)
                if not last:
                    for n in (2, 3):
                        for t in range(2):
                            qk(i + 1, n, t)
                if not first:
                    logits(i - 1)
                if not last:
                    v(i + 1, 0)
                if not first:
                    logits_back(i - 1)
                prob_transposes(i, last)
                if last:
                    places(i - 1)
                context(i, 0)
                if not first and not last:
                    places(i - 1)
                context(i, 1)
                if more:
                    x_transposes(i + 2)
                for j in range(2):
                    for c in range(KC):
                        output(i, 0, j, (c,))

            pe.wait_ge(w_low, 4)
            x_transposes(0)
            pe.wait_ge(su_act, 6)
            for n in range(4):
                for t in range(2):
                    qk(0, n, t)
            for jj in range(2):
                v(0, jj)
            x_transposes(1)
            body(0, first=True)
            with pe.Fori(1, NBLK - 2) as i:
                body(i)
            body(NBLK - 2, more=False)
            body(NBLK - 1, more=False, last=True)
            for j in range(2):
                output(NBLK - 1, 1, j)
            row_transposes(NBLK - 1)
            logits(NBLK - 1)
            logits_back(NBLK - 1)
            places(NBLK - 1)
            pe.wait_ge(rt, RT * NBLK)
            pe.matmul(RB[:, 0:E], ones[:, :], runb[:, :], start=True, stop=True).then_inc(cnt_ps, 1)

            def group_transposes(g):
                b, q = g.buf(2), g.buf(NI)
                pe.wait_ge(g_in[q], 16 * g.before(NI) + 16)
                if g.since(2):
                    pe.wait_ge(gT_done, g.n - 1)
                for c in range(KC):
                    for s in range(GS):
                        mm = pe.transpose(GTB[b][:, c * GT + s * P:c * GT + (s + 1) * P], gin[q][:, s, c * P:(c + 1) * P], ident[:, :])
                mm.then_inc(gT_ps, 1)

            def layer1(g):
                b = g.buf(2)
                pe.wait_ge(gT_done, g.n + 1)
                pe.wait_ge(w_cur, g.n + 1)
                if g.since(2):
                    pe.wait_ge(m_done, 2 * (g.n - 1))
                for m in range(2):
                    for c in range(KC):
                        mm = pe.matmul(MB[b][:, m * GT:(m + 1) * GT], wc[b][:, c, m * P:(m + 1) * P], gT[b][:, c, :],
                                       start=(c == 0), stop=(c == KC - 1))
                mm.then_inc(m_ps, 1)

            def layer2(g):
                b = g.buf(2)
                pe.wait_ge(m_done, 2 * g.n + 2)
                e = pe.value_load(tab[0:1, 1, bass.ds(g.n, 1)], min_val=0, max_val=E - 1)
                if g.since(2):
                    pe.wait_ge(y_read, g.n - 1)
                for s in range(GS):
                    for c in range(2):
                        mm = pe.matmul(YB[b][:, s * D:(s + 1) * D], mT[b][:, c, s * P:(s + 1) * P], we[:, bass.ds(e, 1), 2 + c, :].rearrange("p o f -> p (o f)"),
                                       start=(c == 0), stop=(c == 1))
                mm.then_inc(y_ps, 1)

            def pe_step(g):
                group_transposes(g.plus(2))
                layer1(g.plus(1))
                layer2(g)

            pe.wait_ge(tab_done, 1)
            pe.wait_ge(experts_in, 16 * EXPERT_LOADS)
            group_transposes(Group(0, 0))
            group_transposes(Group(0, 1))
            layer1(Group(0, 0))
            for n in range(3):
                pe_step(Group(0, n))
            for_groups(pe, 3, NG - 3, pe_step)
            layer1(Group(0, NG - 1))
            layer2(Group(0, NG - 2))
            layer2(Group(0, NG - 1))


_INS = ["x", "adj", "L0_gnn_Wq", "L0_gnn_bq", "L0_gnn_Wk", "L0_gnn_bk", "L0_gnn_Wv", "L0_gnn_bv", "L0_gnn_Wo", "L0_gnn_bo",
        "L0_ffn_Wg", "L0_ffn_W1", "L0_ffn_b1", "L0_ffn_W2", "L0_ffn_b2", "L0_ffn_gamma", "L0_ffn_beta"]
_OUTS = [((128, 64, 256), "float32")]


def kernel(**inputs):
    import numpy as _np
    import concourse.bacc as _bacc
    from concourse import mybir as _mybir
    from concourse.bass_utils import run_bass_kernel_spmd as _run

    nc = _bacc.Bacc("TRN2", target_bir_lowering=False, num_devices=1)
    arrays, args = {}, []
    for name in _INS:
        a = _np.ascontiguousarray(inputs[name])
        arrays[f"in_{name}_dram"] = a
        args.append(nc.dram_tensor(f"in_{name}_dram", a.shape, _mybir.dt.from_np(a.dtype), kind="ExternalInput").ap())
    for i, (shape, dtype) in enumerate(_OUTS):
        dt = _mybir.dt.from_np(_np.dtype(dtype))
        args.append(nc.dram_tensor(f"out_{i}_dram", shape, dt, kind="ExternalOutput").ap())
    gnn_moe_layer_kernel(nc, *args)
    r = _run(nc, [arrays], core_ids=[0])
    got = tuple(r.results[0][f"out_{i}_dram"] for i in range(len(_OUTS)))
    return got[0]
```
